# Optimizing a Trainium2 kernel written in Bass

```python
import numpy as np
import jax
import jax.numpy as jnp

def _softmax(x, axis=-1):
    return jax.nn.softmax(x, axis=axis)

def _gelu(x):
    return jax.nn.gelu(x, approximate=True)

def _silu(x):
    return jax.nn.silu(x)

def _sigmoid(x):
    return jax.nn.sigmoid(x)

def _layernorm(x, axis=-1, eps=1e-05):
    m = jnp.mean(x, axis=axis, keepdims=True)
    v = jnp.var(x, axis=axis, keepdims=True)
    return (x - m) / jnp.sqrt(v + eps)

def _scatter_add(tgt, idx, src, axis=0):
    return tgt.at[idx].add(src)

def _segment_sum(src, seg, n):
    return jax.ops.segment_sum(src, seg, n)
kernel_name = 'mk_gnn_resnorm_d1_gnn_r64_7cd2ed'

def setup_inputs(seed: int=0):
    np.random.seed(seed)
    _w = jnp.asarray

    def _rec_inputs():
        import jax
        import jax.numpy as jnp
        _gk = jax.random.key(seed)
        x = -0.0001006 + 1 * jax.random.normal(jax.random.fold_in(_gk, 1), (100000, 96), jnp.float32)
        src = jax.random.randint(jax.random.fold_in(_gk, 2), (25000,), 0, 100000, jnp.int32)
        dst = jnp.minimum((100000 * jax.random.uniform(jax.random.fold_in(_gk, 3), (25000,)) ** 2.0).astype(jnp.int32), 99999)
        _o = jnp.argsort(dst, stable=True)
        src = src[_o]
        dst = dst[_o]
        edge_attr_32 = 0.000196303 + 1.00016 * jax.random.normal(jax.random.fold_in(_gk, 11), (25000, 32), jnp.float32)
        return (x, src, dst, edge_attr_32)
    x, src, dst, edge_attr_32 = _rec_inputs()

    def _L0_gnn_setup():
        import jax, jax.numpy as jnp
        import numpy as np
        N, E = (50000, 12500)
        DIN = DOUT = 96
        DE = 32

        def _egnn_conv(x, src, dst, edge_attr, W_msg, W_edge, W_root, b):
            msg = x[src] @ W_msg + edge_attr @ W_edge
            agg = jax.ops.segment_max(msg, dst, num_segments=x.shape[0])
            agg = jnp.where(jnp.isneginf(agg), 0.0, agg)
            return agg + x @ W_root + b
        key = jax.random.key(seed)
        ks = jax.random.split(key, 10)
        rn = lambda k, sh, sc: jax.random.normal(k, sh, jnp.float32) * sc
        return {'X': rn(ks[0], (N, DIN), 1.0), 'edge_index': jax.random.randint(ks[1], (2, E), 0, N, jnp.int32), 'edge_attr': rn(ks[2], (E, DE), 1.0), 'W1_msg': rn(ks[3], (DIN, DOUT), DIN ** (-0.5)), 'W1_edge': rn(ks[4], (DE, DOUT), DE ** (-0.5)), 'W1_root': rn(ks[5], (DIN, DOUT), DIN ** (-0.5)), 'b1': jnp.zeros((DOUT,), jnp.float32), 'W2_msg': rn(ks[6], (DOUT, DOUT), DOUT ** (-0.5)), 'W2_edge': rn(ks[7], (DE, DOUT), DE ** (-0.5)), 'W2_root': rn(ks[8], (DOUT, DOUT), DOUT ** (-0.5)), 'b2': jnp.zeros((DOUT,), jnp.float32)}
    _L0_gnn_all = _L0_gnn_setup()
    _L0_gnn_in = {k: v for k, v in _L0_gnn_all.items() if k in ('W1_msg', 'W1_edge', 'W1_root', 'b1', 'W2_msg', 'W2_edge', 'W2_root', 'b2')}
    del _L0_gnn_all
    return {'x': x, 'src': src, 'dst': dst, 'edge_attr_32': edge_attr_32, 'L0_gnn_W1_msg': _L0_gnn_in['W1_msg'], 'L0_gnn_W1_edge': _L0_gnn_in['W1_edge'], 'L0_gnn_W1_root': _L0_gnn_in['W1_root'], 'L0_gnn_b1': _L0_gnn_in['b1'], 'L0_gnn_W2_msg': _L0_gnn_in['W2_msg'], 'L0_gnn_W2_edge': _L0_gnn_in['W2_edge'], 'L0_gnn_W2_root': _L0_gnn_in['W2_root'], 'L0_gnn_b2': _L0_gnn_in['b2']}

def reference(x, src, dst, edge_attr_32, L0_gnn_W1_msg, L0_gnn_W1_edge, L0_gnn_W1_root, L0_gnn_b1, L0_gnn_W2_msg, L0_gnn_W2_edge, L0_gnn_W2_root, L0_gnn_b2):
    import jax
    import jax.numpy as jnp

    def _L0_gnn_ref(X, edge_index, edge_attr, W1_msg, W1_edge, W1_root, b1, W2_msg, W2_edge, W2_root, b2):
        import jax, jax.numpy as jnp
        import numpy as np
        N, E = (50000, 12500)
        DIN = DOUT = 96
        DE = 32

        def _egnn_conv(x, src, dst, edge_attr, W_msg, W_edge, W_root, b):
            msg = x[src] @ W_msg + edge_attr @ W_edge
            agg = jax.ops.segment_max(msg, dst, num_segments=x.shape[0])
            agg = jnp.where(jnp.isneginf(agg), 0.0, agg)
            return agg + x @ W_root + b
        src, dst = (edge_index[0], edge_index[1])
        c1 = jax.nn.leaky_relu(_egnn_conv(X, src, dst, edge_attr, W1_msg, W1_edge, W1_root, b1))
        c2 = jax.nn.leaky_relu(_egnn_conv(c1, src, dst, edge_attr, W2_msg, W2_edge, W2_root, b2))
        return c2
    edge_index = jnp.stack([src, dst])
    x = _layernorm(x + _L0_gnn_ref(x, edge_index, edge_attr_32, L0_gnn_W1_msg, L0_gnn_W1_edge, L0_gnn_W1_root, L0_gnn_b1, L0_gnn_W2_msg, L0_gnn_W2_edge, L0_gnn_W2_root, L0_gnn_b2), axis=-1)
    return x

_drawn_inputs = setup_inputs


def setup_inputs(seed=0):
    import zlib

    import numpy as np

    out = dict(_drawn_inputs(seed))
    spreads = {'L0_gnn_b1': (0.0, 0.1), 'L0_gnn_b2': (0.0, 0.1)}
    factors = {}
    for name, (base, spread) in spreads.items():
        noise = np.random.default_rng([zlib.crc32(name.encode()), seed]).standard_normal(out[name].shape)
        drawn = base * np.exp(spread * noise) if base else spread * noise
        out[name] = jnp.asarray(drawn.astype(out[name].dtype))
    for name, factor in factors.items():
        out[name] = (out[name] * factor).astype(out[name].dtype)
    return out
```

```python
from contextlib import ExitStack

import concourse.bass as bass
from concourse import mybir

N, E, D, DE = 100000, 25000, 96, 32
P = 128
Q = 4
GE = P * Q
G = -(-E // GE)
EP = G * GE
R = 8
CN = P * R
C = -(-(N + 1) // CN)
NP = C * CN
HR = R // 2
HN = CN // 2
BK = EP // P
FLT_MAX = 3.4028234663852886e38
SLOPE = 0.01
EPS = 1e-5
assert C == 2 * G and G % 2 == 1 and HN == GE and EP > E

ALU = mybir.AluOpType
ACT = mybir.ActivationFunctionType
F32 = mybir.dt.float32
I32 = mybir.dt.int32


class Step:

    def __init__(self, k, o):
        self.n = k * 2 + o
        self.par = o % 2
        self.turn = k + o // 2
        self.least = o + 2 * (k if isinstance(k, int) else 1)

    def past(self, d):
        return self.least > d


def build(nc, xrows, xcols, ea_t, src_q, dst_q, dst_next_q, src_flat, dst_b, dst_prev_b, dst_shift_b,
          w1_msg, w1_edge, w1_root, b1, w2_msg, w2_edge, w2_root, b2, out):
    with ExitStack() as ctx:
        def sb(name, shape, dt=F32):
            return ctx.enter_context(nc.sbuf_tensor(name, shape, dt))

        def sem(name):
            return ctx.enter_context(nc.semaphore(name))

        def sem2(name):
            return [sem(name + "0"), sem(name + "1")]

        table1 = nc.dram_tensor("table1", [EP + 1, D], F32).ap()
        same_run = nc.dram_tensor("same_run", [EP], F32).ap()
        root_src = nc.dram_tensor("root_src", [G, D, GE], F32).ap()
        h1_dst = nc.dram_tensor("h1_dst", [G, D, GE], F32).ap()

        wm = [sb("wm1", [P, D]), sb("wm2", [P, D])]
        wr1 = sb("wr1", [D, D])
        wr2 = sb("wr2", [D + 1, D])
        b1c = sb("b1c", [D, 1])
        ident = sb("ident", [P, P])
        epsc = sb("epsc", [P, 1])
        zrow = sb("zrow", [1, D])

        srci = sb("srci", [P, G * Q], I32)
        dsti = sb("dsti", [P, G * Q], I32)
        dstn = sb("dstn", [P, G * Q], I32)
        srcf = sb("srcf", [P, G * Q])
        nsrcf = sb("nsrcf", [P, G * Q])
        outf = sb("outf", [P, G * Q])
        outi = sb("outi", [P, G * Q], I32)
        aggi = sb("aggi", [P, G * Q], I32)
        n_le = sb("n_le", [P, G * Q])
        n_sg = sb("n_sg", [P, G * Q])
        n_bk = sb("n_bk", [P, G * Q])
        dstb = sb("dstb", [P, BK], I32)
        dstp = sb("dstp", [P, BK], I32)
        dsts = sb("dsts", [P, BK], I32)
        pivot = sb("pivot", [P, 1])
        steps = sb("steps", [P, BK + 1])
        runs = sb("runs", [P, BK])
        idx_s = sb("idx_s", [P, 2, Q], I32)
        idx_d = sb("idx_d", [P, 2, Q], I32)
        idx_o = sb("idx_o", [P, 2, Q], I32)
        junk_v = sb("junk_v", [P, 2, BK])
        junk_a = sb("junk_a", [P, 2, BK])

        XT = sb("XT", [D, 2, CN])
        H1 = sb("H1", [D + 1, 2, HN])
        C2 = sb("C2", [P, 2, HR, D])
        Y = sb("Y", [P, 2, R, D])
        ST = sb("ST", [P, R, 6])
        MV = sb("MV", [P, 2, R, 2])
        SD = sb("SD", [P, 2, R])
        RS = sb("RS", [P, R])

        XG = sb("XG", [P, 2, Q, D])
        XD = sb("XD", [P, 2, Q, D])
        XS = sb("XS", [P, 2, GE])
        XDT = sb("XDT", [D, 2, GE])
        SB = sb("SB", [P, 2, GE], I32)
        GEQ = sb("GEQ", [P, 2, GE])
        RUN = sb("RUN", [D, 2, GE])
        SC = sb("SC", [D, 2, GE])
        RT = sb("RT", [D, 2, GE])
        HD = sb("HD", [D + 1, 2, GE])
        ROW = sb("ROW", [P, 2, Q, D])
        CE = sb("CE", [P, 2, Q, D])
        YE = sb("YE", [P, G * Q, D])
        STE = sb("STE", [P, Q, 6])
        MVE = sb("MVE", [P, 2, Q, 2])
        SDE = sb("SDE", [P, 2, Q])
        RSE = sb("RSE", [P, Q])
        OUTR = sb("OUTR", [P, 2, Q, D])

        def ps(name):
            return ctx.enter_context(nc.psum_tensor(name, [P, 512], F32))

        p_h1, p_c2, p_x = ps("p_h1"), ps("p_c2"), ps("p_x")
        p_src, p_dst, p_msg, p_row, p_look = ps("p_src"), ps("p_dst"), ps("p_msg"), ps("p_row"), ps("p_look")

        def turned(t):
            return t.rearrange("m (q p) -> m p q", q=Q)

        def in_order(t):
            return t.rearrange("m (p q) -> m p q", q=Q)

        def rows4(t):
            return t[:, 0:Q * D].rearrange("p (q f) -> p q f", q=Q)

        weights_in = sem("weights_in")
        index_in = sem("index_in")
        buckets_in = sem("buckets_in")
        xt_in = sem2("xt_in")
        ea_in = sem2("ea_in")
        run_in = sem2("run_in")
        srcs_in = sem2("srcs_in")
        root_in = sem2("root_in")
        hd_in = sem2("hd_in")
        xg_in = sem2("xg_in")
        xd_in = sem2("xd_in")
        runs_out = sem("runs_out")
        zero_out = sem("zero_out")
        row_out = sem2("row_out")
        root_out = sem2("root_out")
        hd_out = sem2("hd_out")
        y_out = sem2("y_out")
        xd_kept = sem2("xd_kept")
        staged = sem2("staged")
        scattered = sem2("scattered")
        const_set = sem("const_set")
        ident_set = sem("ident_set")
        prep = sem("prep")
        runs_set = sem("runs_set")
        look_set = sem("look_set")
        src_set = sem("src_set")
        outi_set = sem("outi_set")
        aggi_set = sem("aggi_set")
        idx_copied = sem("idx_copied")
        waited_pool = sem("waited_pool")
        waited_dve = sem("waited_dve")
        h1_mm = sem("h1_mm")
        h1_act = sem("h1_act")
        h1_leaky = sem("h1_leaky")
        x_turned = sem("x_turned")
        c2_mm = sem("c2_mm")
        c2_act = sem("c2_act")
        c2_leaky = sem("c2_leaky")
        y_sum = sem("y_sum")
        stats = sem("stats")
        mean_var = sem("mean_var")
        std = sem("std")
        rstd = sem("rstd")
        y_ready = sem("y_ready")
        src_turned = sem("src_turned")
        dst_turned = sem("dst_turned")
        xs_ready = sem("xs_ready")
        xdt_ready = sem("xdt_ready")
        msg_mm = sem("msg_mm")
        root_mm = sem("root_mm")
        rootd_mm = sem("rootd_mm")
        root_act = sem("root_act")
        geq_ready = sem("geq_ready")
        looked = sem("looked")
        le_counted = sem("le_counted")
        sg_counted = sem("sg_counted")
        scanned = sem("scanned")
        hd_sum = sem("hd_sum")
        hd_ready = sem("hd_ready")
        row_turned = sem("row_turned")
        row_ready = sem("row_ready")
        agg_sum = sem("agg_sum")
        c2e_mm = sem("c2e_mm")
        c2e_act = sem("c2e_act")
        c2e_leaky = sem("c2e_leaky")
        ye_sum = sem("ye_sum")
        stats_e = sem("stats_e")
        mean_var_e = sem("mean_var_e")
        std_e = sem("std_e")
        rstd_e = sem("rstd_e")
        ye_ready = sem("ye_ready")

        block = ctx.enter_context(nc.Block())

        def all_groups(eng, slot, first=0):
            slot(0, 0)
            slot(0, 1)
            with eng.Fori(1, G // 2) as k:
                slot(k, 0)
                slot(k, 1)
            slot(G // 2, 0)

        @block.sync
        def _(sp):
            sp.dma_start(srci[:], src_q).then_inc(index_in, 16)
            sp.dma_start(dsti[:], dst_q).then_inc(index_in, 16)
            sp.dma_start(dstn[:], dst_next_q).then_inc(index_in, 16)
            sp.dma_start(dstb[:], dst_b).then_inc(buckets_in, 16)
            sp.dma_start(dstp[:], dst_prev_b).then_inc(buckets_in, 16)
            sp.dma_start(dsts[:], dst_shift_b).then_inc(buckets_in, 16)
            sp.dma_start(wm[0][0:D, :], w1_msg).then_inc(weights_in, 16)
            sp.dma_start(wm[0][D:P, :], w1_edge).then_inc(weights_in, 16)
            sp.dma_start(wm[1][0:D, :], w2_msg).then_inc(weights_in, 16)
            sp.dma_start(wm[1][D:P, :], w2_edge).then_inc(weights_in, 16)
            sp.dma_start(wr1[:], w1_root).then_inc(weights_in, 16)
            sp.dma_start(wr2[0:D, :], w2_root).then_inc(weights_in, 16)
            sp.dma_start(wr2[D:D + 1, :], b2).then_inc(weights_in, 16)
            sp.dma_start(b1c[:], b1).then_inc(weights_in, 16)
            sp.wait_ge(const_set, 1)
            sp.dma_start(table1[EP:EP + 1, :], zrow[:]).then_inc(zero_out, 16)
            sp.wait_ge(runs_set, 1)
            sp.dma_start(same_run.rearrange("(b j) -> b j", b=P), runs[:]).then_inc(runs_out, 16)
            sp.wait_ge(runs_out, 16)

            def load_dense(c):
                if c.past(1):
                    sp.wait_ge(x_turned, c.n * 2 - 2)
                sp.dma_start(XT[:, c.par, :], xcols[:, bass.ds(c.n * CN, CN)]).then_inc(xt_in[c.par], 16)

            def load_edges(s, g):
                if s.past(1):
                    sp.wait_ge(msg_mm, s.n - 1)
                sp.dma_start(XS[D:P, s.par, :], ea_t[:, bass.ds(g.n * GE, GE)]).then_inc(ea_in[s.par], 16)
                if s.past(1):
                    sp.wait_ge(scanned, s.n - 1)
                sp.dma_start(RUN[:, s.par, :], same_run[bass.ds(g.n * GE, GE)].partition_broadcast(D))\
                  .then_inc(run_in[s.par], 16)

            def store_dense(c):
                sp.wait_ge(y_ready, c.n + 1)
                sp.dma_start(out[bass.ds(c.n * CN, CN), :].rearrange("(p r) f -> p (r f)", p=P),
                             Y[:, c.par, :, :].rearrange("p r f -> p (r f)")).then_inc(y_out[c.par], 16)

            def store_a(g):
                sp.wait_ge(xd_in[g.par], (g.turn + 1) * 16 * Q)
                sp.dma_start(YE[:, bass.ds(g.n * Q, Q), :].rearrange("p q f -> p (q f)"),
                             XD[:, g.par, :, :].rearrange("p q f -> p (q f)")).then_inc(xd_kept[g.par], 16)
                sp.wait_ge(root_act, g.n + 1)
                sp.dma_start(root_src[bass.ds(g.n, 1), :, :].rearrange("g d e -> d (g e)"),
                             RT[:, g.par, :]).then_inc(root_out[g.par], 16)
                sp.wait_ge(hd_ready, g.n + 1)
                sp.dma_start(h1_dst[bass.ds(g.n, 1), :, :].rearrange("g d e -> d (g e)"),
                             HD[0:D, g.par, :]).then_inc(hd_out[g.par], 16)
                sp.wait_ge(row_ready, g.n + 1)
                sp.dma_start(table1[bass.ds(g.n * GE, GE), :].rearrange("(p q) f -> p (q f)", p=P),
                             ROW[:, g.par, :, :].rearrange("p q f -> p (q f)")).then_inc(row_out[g.par], 16)

            def slot_a(k, o):
                s = Step(k, o)
                load_dense(s)
                load_edges(s, s)
                if s.past(1):
                    sp.wait_ge(geq_ready, s.n - 1)
                sp.dma_start(SB[:, s.par, :], src_flat[bass.ds(s.n * GE, GE)].partition_broadcast(P))\
                  .then_inc(srcs_in[s.par], 16)
                if s.past(0):
                    before = Step(k, o - 1)
                    store_a(before)
                    if before.past(0):
                        store_dense(Step(k, o - 2))

            all_groups(sp, slot_a)
            last = Step(G // 2, 0)
            store_a(last)
            for par, turns in ((0, G // 2 + 1), (1, G // 2)):
                sp.wait_ge(root_out[par], 16 * turns)
                sp.wait_ge(hd_out[par], 16 * turns)

            def slot_b(k, o):
                s, g = Step(k, o + G), Step(k, o)
                load_dense(s)
                load_edges(s, g)
                if g.past(1):
                    sp.wait_ge(agg_sum, g.n - 1)
                sp.dma_start(RT[:, g.par, :], root_src[bass.ds(g.n, 1), :, :].rearrange("g d e -> d (g e)"))\
                  .then_inc(root_in[g.par], 16)
                if g.past(1):
                    sp.wait_ge(c2e_mm, g.n - 1)
                sp.dma_start(HD[0:D, g.par, :], h1_dst[bass.ds(g.n, 1), :, :].rearrange("g d e -> d (g e)"))\
                  .then_inc(hd_in[g.par], 16)
                store_dense(Step(k, o + G - 2))

            all_groups(sp, slot_b)
            store_dense(Step(G - 1, 0))
            store_dense(Step(G - 1, 1))

            def slot_c(k, o):
                g = Step(k, o)
                sp.wait_ge(ye_ready, g.n + 1)
                if g.past(1):
                    sp.wait_ge(scattered[g.par], g.turn * 16 * Q)
                sp.dma_start(OUTR[:, g.par, :, :].rearrange("p q f -> p (q f)"),
                             YE[:, bass.ds(g.n * Q, Q), :].rearrange("p q f -> p (q f)")).then_inc(staged[g.par], 16)

            all_groups(sp, slot_c)
            for par in (0, 1):
                sp.wait_ge(y_out[par], 16 * G)

        @block.gpsimd
        def _(pool):
            pool.memset(zrow[:], 0.0).then_inc(const_set, 1)
            pool.memset(epsc[:], EPS).then_inc(ident_set, 1)
            pool.memset(ident[:], 0.0).then_inc(ident_set, 1)
            pool.wait_ge(ident_set, 2)
            pool.affine_select(out=ident[:], in_=ident[:], compare_op=ALU.not_equal, fill=1.0, base=0,
                               pattern=[[-1, P]], channel_multiplier=1).then_inc(ident_set, 1)
            pool.wait_ge(index_in, 48)

            def gather(to, rows, idx, par, bound, done):
                for q in range(Q):
                    pool.indirect_dma_start(
                        out=to[:, par, q, :], out_offset=None, in_=rows,
                        in_offset=bass.IndirectOffsetOnAxis(ap=idx[:, par, q:q + 1], axis=0),
                        bounds_check=bound, oob_is_err=False).then_inc(done[par], 16)

            def slot_a(k, o):
                g = Step(k, o)
                if g.past(1):
                    pool.wait_ge(xg_in[g.par], g.turn * 16 * Q)
                    pool.wait_ge(xd_in[g.par], g.turn * 16 * Q)
                pool.tensor_copy(idx_s[:, g.par, :], srci[:, bass.ds(g.n * Q, Q)]).then_inc(idx_copied, 1)
                pool.tensor_copy(idx_d[:, g.par, :], dsti[:, bass.ds(g.n * Q, Q)]).then_inc(idx_copied, 1)
                if g.past(1):
                    pool.wait_ge(src_turned, g.n - 1)
                pool.wait_ge(idx_copied, g.n * 2 + 2)
                pool.sem_inc(waited_pool, 1)
                gather(XG, xrows, idx_s, g.par, NP - 1, xg_in)
                if g.past(1):
                    pool.wait_ge(xd_kept[g.par], g.turn * 16)
                    pool.wait_ge(dst_turned, g.n - 1)
                pool.sem_inc(waited_pool, 1)
                gather(XD, xrows, idx_d, g.par, NP - 1, xd_in)

            all_groups(pool, slot_a)
            for par, turns in ((0, G // 2 + 1), (1, G // 2)):
                pool.wait_ge(row_out[par], 16 * turns)
            pool.wait_ge(zero_out, 16)
            pool.wait_ge(aggi_set, 1)

            def slot_b(k, o):
                s, g = Step(k, o + G), Step(k, o)
                pool.wait_ge(xg_in[s.par], s.turn * 16 * Q)
                pool.tensor_copy(idx_s[:, s.par, :], aggi[:, bass.ds(g.n * Q, Q)]).then_inc(idx_copied, 1)
                pool.wait_ge(idx_copied, g.n + 2 * G + 1)
                pool.wait_ge(src_turned, s.n - 1)
                pool.sem_inc(waited_pool, 1)
                gather(XG, table1, idx_s, s.par, EP, xg_in)

            all_groups(pool, slot_b)
            for par in (0, 1):
                pool.wait_ge(y_out[par], 16 * G)
            pool.wait_ge(outi_set, 1)

            def slot_c(k, o):
                g = Step(k, o)
                if g.past(1):
                    pool.wait_ge(scattered[g.par], g.turn * 16 * Q)
                pool.tensor_copy(idx_o[:, g.par, :], outi[:, bass.ds(g.n * Q, Q)]).then_inc(idx_copied, 1)
                pool.wait_ge(idx_copied, g.n + 3 * G + 1)
                pool.wait_ge(staged[g.par], (g.turn + 1) * 16)
                pool.sem_inc(waited_pool, 1)
                for q in range(Q):
                    pool.indirect_dma_start(
                        out=out, out_offset=bass.IndirectOffsetOnAxis(ap=idx_o[:, g.par, q:q + 1], axis=0),
                        in_=OUTR[:, g.par, q, :], in_offset=None,
                        bounds_check=NP - 1, oob_is_err=False).then_inc(scattered[g.par], 16)

            all_groups(pool, slot_c)
            for par, turns in ((0, G // 2 + 1), (1, G // 2)):
                pool.wait_ge(scattered[par], 16 * Q * turns)

        @block.tensor
        def _(pe):
            pe.wait_ge(weights_in, 128)
            pe.wait_ge(ident_set, 3)

            def h1_half(c, h):
                if h == 0:
                    pe.wait_ge(xt_in[c.par], (c.turn + 1) * 16)
                if c.past(0) or h:
                    pe.wait_ge(h1_act, c.n * 2 + h)
                pe.matmul(p_h1[0:D, :], wr1[:], XT[:, c.par, h * HN:(h + 1) * HN], start=True, stop=True)\
                  .then_inc(h1_mm, 1)

            def c2_half(c, h):
                if c.past(0) or h:
                    pe.wait_ge(y_sum, c.n * 2 + h)
                for r in range(HR):
                    last = pe.transpose(p_x[:, r * D:(r + 1) * D],
                                        XT[:, c.par, h * HN + r * P:h * HN + (r + 1) * P], ident[0:D, 0:D])
                last.then_inc(x_turned, 1)
                pe.wait_ge(h1_leaky, c.n * 2 + h + 1)
                if c.past(0) or h:
                    pe.wait_ge(c2_leaky, c.n * 2 + h)
                for r in range(HR):
                    last = pe.matmul(p_c2[:, r * D:(r + 1) * D], H1[:, h, r * P:(r + 1) * P], wr2[:],
                                     start=True, stop=True)
                last.then_inc(c2_mm, 1)

            def look_up(g, j):
                if g.past(0) or j:
                    pe.wait_ge(le_counted, g.n * 2 + j)
                    pe.wait_ge(sg_counted, g.n * 2 + j)
                for i in range(2):
                    q = 2 * j + i
                    last = pe.matmul(p_look[:, i * (BK + 1):(i + 1) * (BK + 1)], GEQ[:, g.par, q::Q], steps[:],
                                     start=True, stop=True)
                last.then_inc(looked, 1)

            def turn_group(src, par, to, done):
                for q in range(Q):
                    last = pe.transpose(to[0:D, q * P:(q + 1) * P], src[:, par, q, :], ident[:])
                last.then_inc(done, 1)

            def slot_a(k, o):
                g = Step(k, o)
                pe.wait_ge(xg_in[g.par], (g.turn + 1) * 16 * Q)
                if g.past(0):
                    pe.wait_ge(root_act, g.n)
                turn_group(XG, g.par, p_src, src_turned)
                pe.wait_ge(xd_in[g.par], (g.turn + 1) * 16 * Q)
                if g.past(0):
                    pe.wait_ge(hd_sum, g.n)
                turn_group(XD, g.par, p_dst, dst_turned)
                h1_half(g, 0)
                pe.wait_ge(geq_ready, g.n + 1)
                pe.wait_ge(look_set, 1)
                look_up(g, 0)
                pe.wait_ge(xs_ready, g.n + 1)
                pe.wait_ge(ea_in[g.par], (g.turn + 1) * 16)
                if g.past(0):
                    pe.wait_ge(scanned, g.n)
                pe.matmul(p_msg[0:D, :], wm[0][:], XS[:, g.par, :], start=True, stop=True).then_inc(msg_mm, 1)
                pe.matmul(p_src[0:D, :], wr1[:], XS[0:D, g.par, :], start=True, stop=True).then_inc(root_mm, 1)
                pe.wait_ge(xdt_ready, g.n + 1)
                pe.matmul(p_dst[0:D, :], wr1[:], XDT[:, g.par, :], start=True, stop=True).then_inc(rootd_mm, 1)
                c2_half(g, 0)
                h1_half(g, 1)
                look_up(g, 1)
                pe.wait_ge(scanned, g.n + 1)
                if g.past(0):
                    pe.wait_ge(row_ready, g.n)
                for q in range(Q):
                    last = pe.transpose(p_row[:, q * D:(q + 1) * D], SC[:, g.par, q::Q], ident[0:D, 0:D])
                last.then_inc(row_turned, 1)
                c2_half(g, 1)

            all_groups(pe, slot_a)
            pe.wait_ge(root_act, G)
            pe.wait_ge(row_ready, G)

            def slot_b(k, o):
                s, g = Step(k, o + G), Step(k, o)
                pe.wait_ge(xg_in[s.par], (s.turn + 1) * 16 * Q)
                if g.past(0):
                    pe.wait_ge(agg_sum, g.n)
                turn_group(XG, s.par, p_src, src_turned)
                h1_half(s, 0)
                c2_half(s, 0)
                pe.wait_ge(xs_ready, s.n + 1)
                pe.wait_ge(ea_in[s.par], (s.turn + 1) * 16)
                pe.wait_ge(scanned, s.n)
                pe.matmul(p_msg[0:D, :], wm[1][:], XS[:, s.par, :], start=True, stop=True).then_inc(msg_mm, 1)
                h1_half(s, 1)
                c2_half(s, 1)
                pe.wait_ge(scanned, s.n + 1)
                pe.wait_ge(hd_in[g.par], (g.turn + 1) * 16)
                if g.past(0):
                    pe.wait_ge(c2e_leaky, g.n)
                for q in range(Q):
                    to = p_row[:, q * D:(q + 1) * D]
                    pe.matmul(to, HD[:, g.par, q * P:(q + 1) * P], wr2[:], start=True, stop=False)
                    last = pe.matmul(to, SC[:, s.par, q::Q], ident[0:D, 0:D], start=False, stop=True)
                last.then_inc(c2e_mm, 1)

            all_groups(pe, slot_b)

        @block.scalar
        def _(act):
            act.wait_ge(weights_in, 128)
            act.wait_ge(ident_set, 3)
            act.wait_ge(src_set, 1)

            def h1_half(c, h):
                act.wait_ge(h1_mm, c.n * 2 + h + 1)
                if c.past(0):
                    act.wait_ge(c2_mm, c.n * 2 + h - 1)
                act.activation(H1[0:D, h, :], p_h1[0:D, :], ACT.Identity, bias=b1c[:]).then_inc(h1_act, 1)

            def c2_half(c, h):
                act.wait_ge(c2_mm, c.n * 2 + h + 1)
                if c.past(0):
                    act.wait_ge(y_sum, c.n * 2 + h - 1)
                act.activation(C2[:, h, :, :], rows4(p_c2), ACT.Copy, scale=SLOPE).then_inc(c2_act, 1)

            def std_of(c):
                act.wait_ge(mean_var, c.n + 1)
                if c.past(1):
                    act.wait_ge(rstd, c.n - 1)
                act.activation(SD[:, c.par, :], MV[:, c.par, :, 1], ACT.Sqrt, bias=epsc[:]).then_inc(std, 1)

            def signs(g, j):
                act.wait_ge(looked, g.n * 2 + j + 1)
                for i in range(2):
                    t = g.n * Q + 2 * j + i
                    last = act.activation(junk_a[:, i, :], p_look[:, i * (BK + 1):i * (BK + 1) + BK], ACT.Sign,
                                          bias=nsrcf[:, bass.ds(t, 1)], accum_out=n_sg[:, bass.ds(t, 1)])
                last.then_inc(sg_counted, 1)

            def slot_a(k, o):
                g = Step(k, o)
                act.wait_ge(src_turned, g.n + 1)
                if g.past(1):
                    act.wait_ge(root_mm, g.n - 1)
                act.activation(in_order(XS[0:D, g.par, :]), turned(p_src[0:D, :]), ACT.Copy).then_inc(xs_ready, 1)
                act.wait_ge(dst_turned, g.n + 1)
                if g.past(1):
                    act.wait_ge(rootd_mm, g.n - 1)
                act.activation(XDT[:, g.par, :], p_dst[0:D, :], ACT.Copy).then_inc(xdt_ready, 1)
                h1_half(g, 0)
                if g.past(0):
                    std_of(Step(k, o - 1))
                signs(g, 0)
                act.wait_ge(root_mm, g.n + 1)
                if g.past(1):
                    act.wait_ge(root_out[g.par], g.turn * 16)
                act.activation(RT[:, g.par, :], p_src[0:D, :], ACT.Identity, bias=b1c[:]).then_inc(root_act, 1)
                c2_half(g, 0)
                h1_half(g, 1)
                signs(g, 1)
                act.wait_ge(row_turned, g.n + 1)
                if g.past(1):
                    act.wait_ge(row_out[g.par], g.turn * 16)
                act.activation(ROW[:, g.par, :, :], rows4(p_row), ACT.Copy).then_inc(row_ready, 1)
                c2_half(g, 1)

            all_groups(act, slot_a)

            def std_e_of(g):
                act.wait_ge(mean_var_e, g.n + 1)
                if g.past(1):
                    act.wait_ge(rstd_e, g.n - 1)
                act.activation(SDE[:, g.par, :], MVE[:, g.par, :, 1], ACT.Sqrt, bias=epsc[:]).then_inc(std_e, 1)

            def slot_b(k, o):
                s, g = Step(k, o + G), Step(k, o)
                h1_half(s, 0)
                std_of(Step(k, o + G - 1))
                if g.past(1):
                    std_e_of(Step(k, o - 2))
                c2_half(s, 0)
                h1_half(s, 1)
                c2_half(s, 1)
                act.wait_ge(c2e_mm, g.n + 1)
                if g.past(1):
                    act.wait_ge(ye_sum, g.n - 1)
                act.activation(CE[:, g.par, :, :], rows4(p_row), ACT.Copy, scale=SLOPE).then_inc(c2e_act, 1)

            all_groups(act, slot_b)
            std_of(Step(G - 1, 1))
            std_e_of(Step(G // 2 - 1, 1))
            std_e_of(Step(G // 2, 0))

        @block.vector
        def _(dve):
            chained = [0]

            def chain(ins):
                chained[0] += 1
                ins.then_inc(prep, 1)
                dve.wait_ge(prep, chained[0])

            dve.wait_ge(buckets_in, 48)
            chain(dve.tensor_tensor(runs[:], dstb[:], dstp[:], ALU.is_equal))
            chain(dve.tensor_scalar(runs[:], runs[:], 2.0, -1.0, ALU.mult, ALU.add))
            dve.tensor_scalar(runs[:], runs[:], FLT_MAX, None, ALU.mult).then_inc(runs_set, 1)
            dve.wait_ge(index_in, 48)
            dve.tensor_copy(srcf[:], srci[:])
            dve.tensor_scalar(nsrcf[:], srci[:], -1.0, None, ALU.mult).then_inc(src_set, 1)
            chain(dve.tensor_copy(pivot[:], dstb[:, 0:1]))
            chain(dve.memset(pivot[0:1, :], -1.0))
            chain(dve.tensor_tensor(steps[:, 0:BK], dstb[:], dsts[:], ALU.subtract))
            chain(dve.memset(steps[:, BK:BK + 1], float(BK)))
            dve.memset(steps[0:1, BK:BK + 1], 0.0).then_inc(look_set, 1)
            chain(dve.tensor_tensor(outf[:], dsti[:], dstn[:], ALU.is_equal))
            dve.scalar_tensor_tensor(out=outi[:], in0=outf[:], scalar=float(1 << 20), in1=dsti[:],
                                     op0=ALU.mult, op1=ALU.add).then_inc(outi_set, 1)
            dve.memset(H1[D:D + 1, :, :], 1.0)
            chain(dve.memset(HD[D:D + 1, :, :], 1.0))

            def leaky(t):
                return dve.scalar_tensor_tensor(out=t, in0=t, scalar=SLOPE, in1=t, op0=ALU.mult, op1=ALU.max)

            def h1_half(c, h):
                dve.wait_ge(h1_act, c.n * 2 + h + 1)
                leaky(H1[0:D, h, :]).then_inc(h1_leaky, 1)

            def c2_half(c, h):
                dve.wait_ge(c2_act, c.n * 2 + h + 1)
                dve.tensor_tensor(C2[:, h, :, :], rows4(p_c2), C2[:, h, :, :], ALU.max).then_inc(c2_leaky, 1)

            def y_half(c, h):
                dve.wait_ge(c2_leaky, c.n * 2 + h + 1)
                dve.wait_ge(x_turned, c.n * 2 + h + 1)
                if h == 0 and c.past(1):
                    dve.wait_ge(y_out[c.par], c.turn * 16)
                dve.tensor_tensor(Y[:, c.par, h * HR:(h + 1) * HR, :], rows4(p_x), C2[:, h, :, :], ALU.add)\
                   .then_inc(y_sum, 1)

            def stats_of(c):
                if c.past(0):
                    dve.wait_ge(mean_var, c.n)
                dve.wait_ge(y_sum, c.n * 2 + 2)
                dve.sem_inc(waited_dve, 1)
                for r in range(R):
                    last = dve.bn_stats(ST[:, r, :], Y[:, c.par, r, :])
                last.then_inc(stats, 1)
                dve.wait_ge(stats, c.n + 1)
                dve.sem_inc(waited_dve, 1)
                for r in range(R):
                    last = dve.bn_aggr(MV[:, c.par, r, :], ST[:, r, :])
                last.then_inc(mean_var, 1)

            def normalise(c):
                dve.wait_ge(std, c.n + 1)
                dve.reciprocal(RS[:], SD[:, c.par, :]).then_inc(rstd, 1)
                dve.wait_ge(rstd, c.n + 1)
                for r in range(R):
                    y = Y[:, c.par, r, :]
                    last = dve.tensor_scalar(y, y, MV[:, c.par, r, 0:1], RS[:, r:r + 1], ALU.subtract, ALU.mult)
                last.then_inc(y_ready, 1)

            def counts(g, j):
                dve.wait_ge(looked, g.n * 2 + j + 1)
                dve.wait_ge(sg_counted, g.n * 2 + j + 1)
                for i in range(2):
                    t = g.n * Q + 2 * j + i
                    at = i * (BK + 1)
                    dve.tensor_scalar(junk_v[:, i, :], p_look[:, at:at + BK], srcf[:, bass.ds(t, 1)], 0.0, ALU.is_le,
                                      ALU.add, accum_out=n_le[:, bass.ds(t, 1)])
                    last = dve.tensor_copy(n_bk[:, bass.ds(t, 1)], p_look[:, at + BK:at + BK + 1])
                last.then_inc(le_counted, 1)

            def scan(s, first):
                dve.wait_ge(msg_mm, s.n + 1)
                dve.wait_ge(run_in[s.par], (s.turn + 1) * 16)
                start = -FLT_MAX if first else SC[:, 1 - s.par, GE - 1:GE]
                if s.past(0):
                    dve.wait_ge(scanned, s.n)
                dve.tensor_tensor_scan(SC[:, s.par, :], RUN[:, s.par, :], p_msg[0:D, :], start, ALU.min, ALU.max)\
                   .then_inc(scanned, 1)

            def slot_a(k, o):
                g = Step(k, o)
                dve.wait_ge(srcs_in[g.par], (g.turn + 1) * 16)
                if g.past(1):
                    dve.wait_ge(looked, g.n * 2 - 2)
                dve.tensor_scalar(GEQ[:, g.par, :], SB[:, g.par, :], pivot[:], None, ALU.is_ge)\
                   .then_inc(geq_ready, 1)
                h1_half(g, 0)
                counts(g, 0)
                if g.past(1):
                    dve.wait_ge(row_turned, g.n - 1)
                scan(g, isinstance(g.n, int) and g.n == 0)
                c2_half(g, 0)
                y_half(g, 0)
                dve.wait_ge(rootd_mm, g.n + 1)
                dve.wait_ge(scanned, g.n + 1)
                if g.past(1):
                    dve.wait_ge(hd_out[g.par], g.turn * 16)
                dve.scalar_tensor_tensor(
                    out=HD[0:D, g.par, :].rearrange("m (q p) -> m q p", q=Q),
                    in0=p_dst[0:D, :].rearrange("m (q p) -> m q p", q=Q), scalar=b1c[:],
                    in1=SC[:, g.par, :].rearrange("m (p q) -> m q p", q=Q),
                    op0=ALU.add, op1=ALU.add).then_inc(hd_sum, 1)
                h1_half(g, 1)
                counts(g, 1)
                dve.wait_ge(hd_sum, g.n + 1)
                leaky(HD[0:D, g.par, :]).then_inc(hd_ready, 1)
                c2_half(g, 1)
                if g.past(0):
                    normalise(Step(k, o - 1))
                y_half(g, 1)
                stats_of(g)

            all_groups(dve, slot_a)

            dve.wait_ge(sg_counted, 2 * G)
            dve.wait_ge(le_counted, 2 * G)
            found, last = outf, srcf
            chain(dve.scalar_tensor_tensor(out=found[:], in0=n_le[:], scalar=2.0, in1=n_sg[:], op0=ALU.mult, op1=ALU.add))
            chain(dve.tensor_scalar(found[:], found[:], float(BK), None, ALU.is_gt))
            chain(dve.tensor_tensor(last[:], n_le[:], n_bk[:], ALU.add))
            chain(dve.tensor_scalar(last[:], last[:], float(-1 - EP), None, ALU.add))
            chain(dve.tensor_tensor(last[:], last[:], found[:], ALU.mult))
            dve.tensor_scalar(aggi[:], last[:], float(EP), None, ALU.add).then_inc(aggi_set, 1)
            for par, turns in ((0, G // 2 + 1), (1, G // 2)):
                dve.wait_ge(xd_kept[par], 16 * turns)
            dve.wait_ge(root_mm, G)
            dve.wait_ge(row_turned, G)

            def ye(g):
                return YE[:, bass.ds(g.n * Q, Q), :]

            def normalise_e(g):
                dve.wait_ge(std_e, g.n + 1)
                dve.reciprocal(RSE[:], SDE[:, g.par, :]).then_inc(rstd_e, 1)
                dve.wait_ge(rstd_e, g.n + 1)
                for q in range(Q):
                    y = YE[:, bass.ds(g.n * Q + q, 1), :]
                    last = dve.tensor_scalar(y, y, MVE[:, g.par, q, 0:1], RSE[:, q:q + 1], ALU.subtract, ALU.mult)
                last.then_inc(ye_ready, 1)

            def leaky_e(g):
                dve.wait_ge(c2e_act, g.n + 1)
                dve.tensor_tensor(CE[:, g.par, :, :], rows4(p_row), CE[:, g.par, :, :], ALU.max)\
                   .then_inc(c2e_leaky, 1)

            def sum_e(g):
                dve.wait_ge(c2e_leaky, g.n + 1)
                dve.tensor_tensor(ye(g), ye(g), CE[:, g.par, :, :], ALU.add).then_inc(ye_sum, 1)
                if g.past(0):
                    dve.wait_ge(mean_var_e, g.n)
                dve.wait_ge(ye_sum, g.n + 1)
                dve.sem_inc(waited_dve, 1)
                for q in range(Q):
                    last = dve.bn_stats(STE[:, q, :], YE[:, bass.ds(g.n * Q + q, 1), :])
                last.then_inc(stats_e, 1)
                dve.wait_ge(stats_e, g.n + 1)
                dve.sem_inc(waited_dve, 1)
                for q in range(Q):
                    last = dve.bn_aggr(MVE[:, g.par, q, :], STE[:, q, :])
                last.then_inc(mean_var_e, 1)

            def slot_b(k, o):
                s, g = Step(k, o + G), Step(k, o)
                dve.wait_ge(src_turned, s.n + 1)
                dve.wait_ge(root_in[g.par], (g.turn + 1) * 16)
                dve.wait_ge(msg_mm, s.n - 1)
                dve.tensor_tensor(in_order(XS[0:D, s.par, :]), turned(p_src[0:D, :]), in_order(RT[:, g.par, :]),
                                  ALU.add).then_inc(agg_sum, 1)
                h1_half(s, 0)
                dve.wait_ge(agg_sum, g.n + 1)
                leaky(XS[0:D, s.par, :]).then_inc(xs_ready, 1)
                c2_half(s, 0)
                if g.past(1):
                    normalise_e(Step(k, o - 2))
                y_half(s, 0)
                h1_half(s, 1)
                if g.past(1):
                    dve.wait_ge(c2e_mm, g.n - 1)
                scan(s, isinstance(g.n, int) and g.n == 0)
                c2_half(s, 1)
                normalise(Step(k, o + G - 1))
                y_half(s, 1)
                if g.past(0):
                    leaky_e(Step(k, o - 1))
                stats_of(s)
                if g.past(0):
                    sum_e(Step(k, o - 1))

            all_groups(dve, slot_b)
            normalise(Step(G - 1, 1))
            normalise_e(Step(G // 2 - 1, 1))
            leaky_e(Step(G // 2, 0))
            sum_e(Step(G // 2, 0))
            normalise_e(Step(G // 2, 0))


def kernel(x, src, dst, edge_attr_32, L0_gnn_W1_msg, L0_gnn_W1_edge, L0_gnn_W1_root, L0_gnn_b1,
           L0_gnn_W2_msg, L0_gnn_W2_edge, L0_gnn_W2_root, L0_gnn_b2):
    import numpy as np
    import concourse.bacc as bacc
    from concourse.bass_utils import run_bass_kernel_spmd as run

    x, src, dst, ea = (np.asarray(a) for a in (x, src, dst, edge_attr_32))
    xrows = np.zeros((NP, D), x.dtype)
    xrows[:N] = x
    xcols = xrows.reshape(C, P, 2, HR, D).transpose(4, 0, 2, 3, 1).reshape(D, NP)
    ea_t = np.zeros((DE, EP), ea.dtype)
    ea_t[:, :E] = ea.T
    src_p = np.zeros(EP, src.dtype)
    src_p[:E] = src
    dst_p = np.full(EP + 1, N, dst.dtype)
    dst_p[:E] = dst
    dst_p[EP] = N + 1
    before = np.concatenate([np.full(1, -1, dst.dtype), dst_p[:EP - 1]])

    def by_group(a):
        return a.reshape(G, P, Q).transpose(1, 0, 2).reshape(P, G * Q)

    buckets = dst_p[:EP].reshape(P, BK)
    shifted = np.concatenate([np.zeros((1, BK), dst.dtype), buckets[:-1]])
    arrays = {
        "xrows": xrows, "xcols": xcols, "ea_t": ea_t,
        "src_q": by_group(src_p), "dst_q": by_group(dst_p[:EP]), "dst_next_q": by_group(dst_p[1:]),
        "src_flat": src_p, "dst_b": buckets, "dst_prev_b": before.reshape(P, BK), "dst_shift_b": shifted,
        "w1_msg": L0_gnn_W1_msg, "w1_edge": L0_gnn_W1_edge, "w1_root": L0_gnn_W1_root,
        "b1": np.asarray(L0_gnn_b1).reshape(D, 1),
        "w2_msg": L0_gnn_W2_msg, "w2_edge": L0_gnn_W2_edge, "w2_root": L0_gnn_W2_root,
        "b2": np.asarray(L0_gnn_b2).reshape(1, D),
    }
    nc = bacc.Bacc("TRN2", target_bir_lowering=False, num_devices=1)
    sent, args = {}, []
    for name, a in arrays.items():
        a = np.ascontiguousarray(a)
        sent[f"in_{name}"] = a
        args.append(nc.dram_tensor(f"in_{name}", a.shape, mybir.dt.from_np(a.dtype), kind="ExternalInput").ap())
    out = nc.dram_tensor("out_rows", (NP, D), F32, kind="ExternalOutput").ap()
    build(nc, *args, out)
    r = run(nc, [sent], core_ids=[0])
    return r.results[0]["out_rows"][:N]
```

```python
from contextlib import ExitStack

import concourse.bass as bass
from concourse import mybir

N, E, D, DE = 100000, 25000, 96, 32
P = 128
Q = 4
GE = P * Q
G = -(-E // GE)
EP = G * GE
R = 8
CN = P * R
C = -(-(N + 1) // CN)
NP = C * CN
HR = R // 2
HN = CN // 2
BK = EP // P
FLT_MAX = 3.4028234663852886e38
SLOPE = 0.01
EPS = 1e-5
assert C == 2 * G and G % 2 == 1 and HN == GE and EP > E

ALU = mybir.AluOpType
ACT = mybir.ActivationFunctionType
F32 = mybir.dt.float32
I32 = mybir.dt.int32


class Step:

    def __init__(self, k, o, k0=None):
        self.k, self.o, self.k0 = k, o, k if k0 is None else k0
        self.n = k * 2 + o
        self.par = o % 2
        self.turn = k + o // 2
        self.looped = k0 is not None

    def shift(self, d):
        return Step(self.k, self.o + d, self.k0 if self.looped else None)

    def past(self, d):
        return 2 * self.k0 + self.o > d

    def within(self, count):
        return self.looped or 0 <= self.n < count


def build(nc, xrows, xcols, ea_t, src_q, dst_q, dst_next_q, src_flat, dst_b, dst_prev_b, dst_shift_b,
          w1_msg, w1_edge, w1_root, b1, w2_msg, w2_edge, w2_root, b2, out):
    with ExitStack() as ctx:
        def sb(name, shape, dt=F32):
            return ctx.enter_context(nc.sbuf_tensor(name, shape, dt))

        def sem(name):
            return ctx.enter_context(nc.semaphore(name))

        def sem2(name):
            return [sem(name + "0"), sem(name + "1")]

        table1 = nc.dram_tensor("table1", [EP + 1, D], F32).ap()
        same_run = nc.dram_tensor("same_run", [EP], F32).ap()
        root_src = nc.dram_tensor("root_src", [G, D, GE], F32).ap()
        h1_dst = nc.dram_tensor("h1_dst", [G, D, GE], F32).ap()

        wm = [sb("wm1", [P, D]), sb("wm2", [P, D])]
        wr1 = sb("wr1", [D, D])
        wr2 = sb("wr2", [D + 1, D])
        b1c = sb("b1c", [D, 1])
        ident = sb("ident", [P, P])
        epsc = sb("epsc", [P, 1])
        zrow = sb("zrow", [1, D])

        srci = sb("srci", [P, G * Q], I32)
        dsti = sb("dsti", [P, G * Q], I32)
        dstn = sb("dstn", [P, G * Q], I32)
        srcf = sb("srcf", [P, G * Q])
        nsrcf = sb("nsrcf", [P, G * Q])
        outf = sb("outf", [P, G * Q])
        outi = sb("outi", [P, G * Q], I32)
        aggi = sb("aggi", [P, G * Q], I32)
        n_le = sb("n_le", [P, G * Q])
        n_sg = sb("n_sg", [P, G * Q])
        n_bk = sb("n_bk", [P, G * Q])
        dstb = sb("dstb", [P, BK], I32)
        dstp = sb("dstp", [P, BK], I32)
        dsts = sb("dsts", [P, BK], I32)
        pivot = sb("pivot", [P, 1])
        steps = sb("steps", [P, BK + 1])
        runs = sb("runs", [P, BK])
        idx_s = sb("idx_s", [P, 2, Q], I32)
        idx_d = sb("idx_d", [P, 2, Q], I32)
        idx_o = sb("idx_o", [P, 2, Q], I32)
        junk_v = sb("junk_v", [P, 2, BK])
        junk_a = sb("junk_a", [P, 2, BK])

        XT = sb("XT", [D, 2, CN])
        H1 = sb("H1", [D + 1, 2, HN])
        C2 = sb("C2", [P, 2, HR, D])
        Y = sb("Y", [P, 2, R, D])
        ST = sb("ST", [P, R, 6])
        MV = sb("MV", [P, 2, R, 2])
        SD = sb("SD", [P, 2, R])
        RS = sb("RS", [P, 2, R])
        NM = sb("NM", [P, 2, R])

        XG = sb("XG", [P, 2, Q, D])
        XD = sb("XD", [P, 2, Q, D])
        XS = sb("XS", [P, 2, GE])
        XDT = sb("XDT", [D, 2, GE])
        SB = sb("SB", [P, 2, GE], I32)
        GEQ = sb("GEQ", [P, 2, GE])
        RUN = sb("RUN", [D, 2, GE])
        SC = sb("SC", [D, 2, GE])
        RT = sb("RT", [D, 2, GE])
        HD = sb("HD", [D + 1, 2, GE])
        ROW = sb("ROW", [P, 2, Q, D])
        CE = sb("CE", [P, 2, Q, D])
        YE = sb("YE", [P, G * Q, D])
        STE = sb("STE", [P, Q, 6])
        MVE = sb("MVE", [P, 2, Q, 2])
        SDE = sb("SDE", [P, 2, Q])
        RSE = sb("RSE", [P, Q])
        OUTR = sb("OUTR", [P, 2, Q, D])

        def ps(name):
            return ctx.enter_context(nc.psum_tensor(name, [P, 512], F32))

        p_h1, p_c2, p_x = ps("p_h1"), ps("p_c2"), ps("p_x")
        p_src, p_dst, p_msg, p_row, p_look = ps("p_src"), ps("p_dst"), ps("p_msg"), ps("p_row"), ps("p_look")

        def turned(t):
            return t.rearrange("m (q p) -> m p q", q=Q)

        def in_order(t):
            return t.rearrange("m (p q) -> m p q", q=Q)

        def rows4(t):
            return t[:, 0:Q * D].rearrange("p (q f) -> p q f", q=Q)

        weights_in = sem("weights_in")
        index_in = sem("index_in")
        buckets_in = sem("buckets_in")
        xt_in = sem2("xt_in")
        ea_in = sem2("ea_in")
        run_in = sem2("run_in")
        srcs_in = sem2("srcs_in")
        root_in = sem2("root_in")
        hd_in = sem2("hd_in")
        xg_in = sem2("xg_in")
        xd_in = sem2("xd_in")
        runs_out = sem("runs_out")
        zero_out = sem("zero_out")
        row_out = sem2("row_out")
        root_out = sem2("root_out")
        hd_out = sem2("hd_out")
        y_out = sem2("y_out")
        xd_kept = sem2("xd_kept")
        staged = sem2("staged")
        scattered = sem2("scattered")
        const_set = sem("const_set")
        ident_set = sem("ident_set")
        prep = sem("prep")
        runs_set = sem("runs_set")
        look_set = sem("look_set")
        src_set = sem("src_set")
        outi_set = sem("outi_set")
        aggi_set = sem("aggi_set")
        idx_copied = sem("idx_copied")
        waited_pool = sem("waited_pool")
        waited_dve = sem("waited_dve")
        h1_mm = sem("h1_mm")
        h1_act = sem("h1_act")
        h1_leaky = sem("h1_leaky")
        x_turned = sem("x_turned")
        c2_mm = sem("c2_mm")
        c2_act = sem("c2_act")
        c2_leaky = sem("c2_leaky")
        y_sum = sem("y_sum")
        stats = sem("stats")
        mean_var = sem("mean_var")
        std = sem("std")
        recip = sem("recip")
        rstd = sem("rstd")
        y_ready = sem("y_ready")
        src_turned = sem("src_turned")
        dst_turned = sem("dst_turned")
        xs_ready = sem("xs_ready")
        xdt_ready = sem("xdt_ready")
        msg_mm = sem("msg_mm")
        root_mm = sem("root_mm")
        rootd_mm = sem("rootd_mm")
        root_act = sem("root_act")
        geq_ready = sem("geq_ready")
        looked = sem("looked")
        le_counted = sem("le_counted")
        sg_counted = sem("sg_counted")
        scanned = sem("scanned")
        hd_sum = sem("hd_sum")
        hd_ready = sem("hd_ready")
        row_turned = sem("row_turned")
        row_ready = sem("row_ready")
        agg_sum = sem("agg_sum")
        c2e_mm = sem("c2e_mm")
        c2e_act = sem("c2e_act")
        c2e_leaky = sem("c2e_leaky")
        ye_sum = sem("ye_sum")
        stats_e = sem("stats_e")
        mean_var_e = sem("mean_var_e")
        std_e = sem("std_e")
        rstd_e = sem("rstd_e")
        ye_ready = sem("ye_ready")

        block = ctx.enter_context(nc.Block())

        def run_slots(eng, slot, ahead, behind):
            for n in range(2 * ahead):
                slot(Step(n // 2, n % 2))
            with eng.Fori(ahead, G // 2) as k:
                slot(Step(k, 0, ahead))
                slot(Step(k, 1, ahead))
            for n in range(G - 1, G + behind):
                slot(Step(n // 2, n % 2))

        @block.sync
        def _(sp):
            sp.dma_start(srci[:], src_q).then_inc(index_in, 16)
            sp.dma_start(dsti[:], dst_q).then_inc(index_in, 16)
            sp.dma_start(dstn[:], dst_next_q).then_inc(index_in, 16)
            sp.dma_start(dstb[:], dst_b).then_inc(buckets_in, 16)
            sp.dma_start(dstp[:], dst_prev_b).then_inc(buckets_in, 16)
            sp.dma_start(dsts[:], dst_shift_b).then_inc(buckets_in, 16)
            sp.dma_start(wm[0][0:D, :], w1_msg).then_inc(weights_in, 16)
            sp.dma_start(wm[0][D:P, :], w1_edge).then_inc(weights_in, 16)
            sp.dma_start(wm[1][0:D, :], w2_msg).then_inc(weights_in, 16)
            sp.dma_start(wm[1][D:P, :], w2_edge).then_inc(weights_in, 16)
            sp.dma_start(wr1[:], w1_root).then_inc(weights_in, 16)
            sp.dma_start(wr2[0:D, :], w2_root).then_inc(weights_in, 16)
            sp.dma_start(wr2[D:D + 1, :], b2).then_inc(weights_in, 16)
            sp.dma_start(b1c[:], b1).then_inc(weights_in, 16)
            sp.wait_ge(const_set, 1)
            sp.dma_start(table1[EP:EP + 1, :], zrow[:]).then_inc(zero_out, 16)
            sp.wait_ge(runs_set, 1)
            sp.dma_start(same_run.rearrange("(b j) -> b j", b=P), runs[:]).then_inc(runs_out, 16)
            sp.wait_ge(runs_out, 16)

            def load_dense(c):
                if c.past(1):
                    sp.wait_ge(x_turned, c.n * 2 - 2)
                sp.dma_start(XT[:, c.par, :], xcols[:, bass.ds(c.n * CN, CN)]).then_inc(xt_in[c.par], 16)

            def load_edges(s, g):
                if s.past(1):
                    sp.wait_ge(msg_mm, s.n - 1)
                sp.dma_start(XS[D:P, s.par, :], ea_t[:, bass.ds(g.n * GE, GE)]).then_inc(ea_in[s.par], 16)
                if s.past(1):
                    sp.wait_ge(scanned, s.n - 1)
                sp.dma_start(RUN[:, s.par, :], same_run[bass.ds(g.n * GE, GE)].partition_broadcast(D))\
                  .then_inc(run_in[s.par], 16)

            def store_dense(c):
                sp.wait_ge(y_ready, c.n + 1)
                sp.dma_start(out[bass.ds(c.n * CN, CN), :].rearrange("(p r) f -> p (r f)", p=P),
                             Y[:, c.par, :, :].rearrange("p r f -> p (r f)")).then_inc(y_out[c.par], 16)

            def store_a(g):
                sp.wait_ge(xd_in[g.par], (g.turn + 1) * 16 * Q)
                sp.dma_start(YE[:, bass.ds(g.n * Q, Q), :].rearrange("p q f -> p (q f)"),
                             XD[:, g.par, :, :].rearrange("p q f -> p (q f)")).then_inc(xd_kept[g.par], 16)
                sp.wait_ge(root_act, g.n + 1)
                sp.dma_start(root_src[bass.ds(g.n, 1), :, :].rearrange("g d e -> d (g e)"),
                             RT[:, g.par, :]).then_inc(root_out[g.par], 16)
                sp.wait_ge(hd_ready, g.n + 1)
                sp.dma_start(h1_dst[bass.ds(g.n, 1), :, :].rearrange("g d e -> d (g e)"),
                             HD[0:D, g.par, :]).then_inc(hd_out[g.par], 16)
                sp.wait_ge(row_ready, g.n + 1)
                sp.dma_start(table1[bass.ds(g.n * GE, GE), :].rearrange("(p q) f -> p (q f)", p=P),
                             ROW[:, g.par, :, :].rearrange("p q f -> p (q f)")).then_inc(row_out[g.par], 16)

            def load_sources(g):
                if g.past(1):
                    sp.wait_ge(geq_ready, g.n - 1)
                sp.dma_start(SB[:, g.par, :], src_flat[bass.ds(g.n * GE, GE)].partition_broadcast(P))\
                  .then_inc(srcs_in[g.par], 16)

            load_dense(Step(0, 0))
            load_sources(Step(0, 0))

            def slot_a(s):
                if s.within(G):
                    load_dense(s.shift(1))
                    load_edges(s, s)
                if s.shift(1).within(G):
                    load_sources(s.shift(1))
                if s.shift(-1).within(G):
                    store_a(s.shift(-1))
                    if s.within(G):
                        store_dense(s.shift(-1))

            run_slots(sp, slot_a, 1, 1)
            for par, turns in ((0, G // 2 + 1), (1, G // 2)):
                sp.wait_ge(root_out[par], 16 * turns)
                sp.wait_ge(hd_out[par], 16 * turns)

            def slot_b(g):
                s = g.shift(G)
                if g.within(G - 1):
                    load_dense(s.shift(1))
                load_edges(s, g)
                if g.past(1):
                    sp.wait_ge(agg_sum, g.n - 1)
                sp.dma_start(RT[:, g.par, :], root_src[bass.ds(g.n, 1), :, :].rearrange("g d e -> d (g e)"))\
                  .then_inc(root_in[g.par], 16)
                if g.past(1):
                    sp.wait_ge(c2e_mm, g.n - 1)
                sp.dma_start(HD[0:D, g.par, :], h1_dst[bass.ds(g.n, 1), :, :].rearrange("g d e -> d (g e)"))\
                  .then_inc(hd_in[g.par], 16)
                store_dense(s.shift(-1))

            run_slots(sp, slot_b, 1, 0)
            store_dense(Step(G - 1, 1))

            def slot_c(g):
                sp.wait_ge(ye_ready, g.n + 1)
                if g.past(1):
                    sp.wait_ge(scattered[g.par], g.turn * 16 * Q)
                sp.dma_start(OUTR[:, g.par, :, :].rearrange("p q f -> p (q f)"),
                             YE[:, bass.ds(g.n * Q, Q), :].rearrange("p q f -> p (q f)")).then_inc(staged[g.par], 16)

            run_slots(sp, slot_c, 1, 0)
            for par in (0, 1):
                sp.wait_ge(y_out[par], 16 * G)

        @block.gpsimd
        def _(pool):
            pool.memset(zrow[:], 0.0).then_inc(const_set, 1)
            pool.memset(epsc[:], EPS).then_inc(ident_set, 1)
            pool.memset(ident[:], 0.0).then_inc(ident_set, 1)
            pool.wait_ge(ident_set, 2)
            pool.affine_select(out=ident[:], in_=ident[:], compare_op=ALU.not_equal, fill=1.0, base=0,
                               pattern=[[-1, P]], channel_multiplier=1).then_inc(ident_set, 1)
            pool.wait_ge(index_in, 48)

            def gather(to, rows, idx, par, bound, done):
                for q in range(Q):
                    pool.indirect_dma_start(
                        out=to[:, par, q, :], out_offset=None, in_=rows,
                        in_offset=bass.IndirectOffsetOnAxis(ap=idx[:, par, q:q + 1], axis=0),
                        bounds_check=bound, oob_is_err=False).then_inc(done[par], 16)

            def slot_a(g):
                if g.past(1):
                    pool.wait_ge(xg_in[g.par], g.turn * 16 * Q)
                    pool.wait_ge(xd_in[g.par], g.turn * 16 * Q)
                pool.tensor_copy(idx_s[:, g.par, :], srci[:, bass.ds(g.n * Q, Q)]).then_inc(idx_copied, 1)
                pool.tensor_copy(idx_d[:, g.par, :], dsti[:, bass.ds(g.n * Q, Q)]).then_inc(idx_copied, 1)
                if g.past(1):
                    pool.wait_ge(src_turned, g.n - 1)
                pool.wait_ge(idx_copied, g.n * 2 + 2)
                pool.sem_inc(waited_pool, 1)
                gather(XG, xrows, idx_s, g.par, NP - 1, xg_in)
                if g.past(1):
                    pool.wait_ge(xd_kept[g.par], g.turn * 16)
                    pool.wait_ge(dst_turned, g.n - 1)
                pool.sem_inc(waited_pool, 1)
                gather(XD, xrows, idx_d, g.par, NP - 1, xd_in)

            run_slots(pool, slot_a, 1, 0)
            for par, turns in ((0, G // 2 + 1), (1, G // 2)):
                pool.wait_ge(row_out[par], 16 * turns)
            pool.wait_ge(zero_out, 16)
            pool.wait_ge(aggi_set, 1)

            def slot_b(g):
                s = g.shift(G)
                pool.wait_ge(xg_in[s.par], s.turn * 16 * Q)
                pool.tensor_copy(idx_s[:, s.par, :], aggi[:, bass.ds(g.n * Q, Q)]).then_inc(idx_copied, 1)
                pool.wait_ge(idx_copied, g.n + 2 * G + 1)
                pool.wait_ge(src_turned, s.n - 1)
                pool.sem_inc(waited_pool, 1)
                gather(XG, table1, idx_s, s.par, EP, xg_in)

            run_slots(pool, slot_b, 1, 0)
            for par in (0, 1):
                pool.wait_ge(y_out[par], 16 * G)
            pool.wait_ge(outi_set, 1)

            def slot_c(g):
                if g.past(1):
                    pool.wait_ge(scattered[g.par], g.turn * 16 * Q)
                pool.tensor_copy(idx_o[:, g.par, :], outi[:, bass.ds(g.n * Q, Q)]).then_inc(idx_copied, 1)
                pool.wait_ge(idx_copied, g.n + 3 * G + 1)
                pool.wait_ge(staged[g.par], (g.turn + 1) * 16)
                pool.sem_inc(waited_pool, 1)
                for q in range(Q):
                    pool.indirect_dma_start(
                        out=out, out_offset=bass.IndirectOffsetOnAxis(ap=idx_o[:, g.par, q:q + 1], axis=0),
                        in_=OUTR[:, g.par, q, :], in_offset=None,
                        bounds_check=NP - 1, oob_is_err=False).then_inc(scattered[g.par], 16)

            run_slots(pool, slot_c, 1, 0)
            for par, turns in ((0, G // 2 + 1), (1, G // 2)):
                pool.wait_ge(scattered[par], 16 * Q * turns)

        @block.tensor
        def _(pe):
            pe.wait_ge(weights_in, 128)
            pe.wait_ge(ident_set, 3)

            def h1_half(c, h):
                if h == 0:
                    pe.wait_ge(xt_in[c.par], (c.turn + 1) * 16)
                if c.past(0) or h:
                    pe.wait_ge(h1_act, c.n * 2 + h)
                pe.matmul(p_h1[0:D, :], wr1[:], XT[:, c.par, h * HN:(h + 1) * HN], start=True, stop=True)\
                  .then_inc(h1_mm, 1)

            def x_half(c, h):
                if c.past(0) or h:
                    pe.wait_ge(y_sum, c.n * 2 + h)
                for r in range(HR):
                    last = pe.transpose(p_x[:, r * D:(r + 1) * D],
                                        XT[:, c.par, h * HN + r * P:h * HN + (r + 1) * P], ident[0:D, 0:D])
                last.then_inc(x_turned, 1)

            def c2_half(c, h):
                pe.wait_ge(h1_leaky, c.n * 2 + h + 1)
                if c.past(0) or h:
                    pe.wait_ge(c2_leaky, c.n * 2 + h)
                for r in range(HR):
                    last = pe.matmul(p_c2[:, r * D:(r + 1) * D], H1[:, h, r * P:(r + 1) * P], wr2[:],
                                     start=True, stop=True)
                last.then_inc(c2_mm, 1)

            def look_up(g, j):
                if g.past(0) or j:
                    pe.wait_ge(le_counted, g.n * 2 + j)
                    pe.wait_ge(sg_counted, g.n * 2 + j)
                for i in range(2):
                    q = 2 * j + i
                    last = pe.matmul(p_look[:, i * (BK + 1):(i + 1) * (BK + 1)], GEQ[:, g.par, q::Q], steps[:],
                                     start=True, stop=True)
                last.then_inc(looked, 1)

            def turn_group(src, par, to, done):
                for q in range(Q):
                    last = pe.transpose(to[0:D, q * P:(q + 1) * P], src[:, par, q, :], ident[:])
                last.then_inc(done, 1)

            h1_half(Step(0, 0), 0)

            def slot_a(s):
                g = s.shift(-1)
                if s.within(G):
                    c2_half(s, 0)
                    h1_half(s, 1)
                if g.within(G):
                    pe.wait_ge(xs_ready, g.n + 1)
                    pe.wait_ge(ea_in[g.par], (g.turn + 1) * 16)
                    if g.past(0):
                        pe.wait_ge(scanned, g.n)
                    pe.matmul(p_msg[0:D, :], wm[0][:], XS[:, g.par, :], start=True, stop=True).then_inc(msg_mm, 1)
                    pe.matmul(p_src[0:D, :], wr1[:], XS[0:D, g.par, :], start=True, stop=True).then_inc(root_mm, 1)
                    pe.wait_ge(xdt_ready, g.n + 1)
                    pe.matmul(p_dst[0:D, :], wr1[:], XDT[:, g.par, :], start=True, stop=True).then_inc(rootd_mm, 1)
                if s.within(G):
                    x_half(s, 0)
                    pe.wait_ge(geq_ready, s.n + 1)
                    pe.wait_ge(look_set, 1)
                    look_up(s, 0)
                    c2_half(s, 1)
                    h1_half(s.shift(1), 0)
                    look_up(s, 1)
                if g.within(G):
                    pe.wait_ge(scanned, g.n + 1)
                    if g.past(0):
                        pe.wait_ge(row_ready, g.n)
                    for q in range(Q):
                        last = pe.transpose(p_row[:, q * D:(q + 1) * D], SC[:, g.par, q::Q], ident[0:D, 0:D])
                    last.then_inc(row_turned, 1)
                if s.within(G):
                    pe.wait_ge(xg_in[s.par], (s.turn + 1) * 16 * Q)
                    if s.past(0):
                        pe.wait_ge(root_act, s.n)
                    turn_group(XG, s.par, p_src, src_turned)
                    pe.wait_ge(xd_in[s.par], (s.turn + 1) * 16 * Q)
                    if s.past(0):
                        pe.wait_ge(hd_sum, s.n)
                    turn_group(XD, s.par, p_dst, dst_turned)
                    x_half(s, 1)

            run_slots(pe, slot_a, 1, 1)
            pe.wait_ge(root_act, G)
            pe.wait_ge(row_ready, G)

            def slot_b(s):
                c, g = s.shift(G), s.shift(-1)
                if s.within(G):
                    c2_half(c, 0)
                    h1_half(c, 1)
                if g.within(G):
                    e = g.shift(G)
                    pe.wait_ge(xs_ready, e.n + 1)
                    pe.wait_ge(ea_in[e.par], (e.turn + 1) * 16)
                    pe.wait_ge(scanned, e.n)
                    pe.matmul(p_msg[0:D, :], wm[1][:], XS[:, e.par, :], start=True, stop=True).then_inc(msg_mm, 1)
                if s.within(G):
                    x_half(c, 0)
                    c2_half(c, 1)
                    if s.within(G - 1):
                        h1_half(c.shift(1), 0)
                    pe.wait_ge(xg_in[c.par], (c.turn + 1) * 16 * Q)
                    if s.past(0):
                        pe.wait_ge(agg_sum, s.n)
                    turn_group(XG, c.par, p_src, src_turned)
                if g.within(G):
                    pe.wait_ge(scanned, e.n + 1)
                    pe.wait_ge(hd_in[g.par], (g.turn + 1) * 16)
                    if g.past(0):
                        pe.wait_ge(c2e_leaky, g.n)
                    for q in range(Q):
                        to = p_row[:, q * D:(q + 1) * D]
                        pe.matmul(to, HD[:, g.par, q * P:(q + 1) * P], wr2[:], start=True, stop=False)
                        last = pe.matmul(to, SC[:, e.par, q::Q], ident[0:D, 0:D], start=False, stop=True)
                    last.then_inc(c2e_mm, 1)
                if s.within(G):
                    x_half(c, 1)

            run_slots(pe, slot_b, 1, 1)

        @block.scalar
        def _(act):
            act.wait_ge(weights_in, 128)
            act.wait_ge(ident_set, 3)
            act.wait_ge(src_set, 1)

            def h1_half(c, h):
                act.wait_ge(h1_mm, c.n * 2 + h + 1)
                if c.past(0):
                    act.wait_ge(c2_mm, c.n * 2 + h - 1)
                act.activation(H1[0:D, h, :], p_h1[0:D, :], ACT.Identity, bias=b1c[:]).then_inc(h1_act, 1)

            def c2_half(c, h):
                act.wait_ge(c2_mm, c.n * 2 + h + 1)
                if c.past(0):
                    act.wait_ge(y_sum, c.n * 2 + h - 1)
                act.activation(C2[:, h, :, :], rows4(p_c2), ACT.Copy, scale=SLOPE).then_inc(c2_act, 1)

            def std_of(c):
                act.wait_ge(mean_var, c.n + 1)
                if c.past(1):
                    act.wait_ge(rstd, c.n - 1)
                act.activation(SD[:, c.par, :], MV[:, c.par, :, 1], ACT.Sqrt, bias=epsc[:]).then_inc(std, 1)

            def signs(g, j):
                act.wait_ge(looked, g.n * 2 + j + 1)
                for i in range(2):
                    t = g.n * Q + 2 * j + i
                    last = act.activation(junk_a[:, i, :], p_look[:, i * (BK + 1):i * (BK + 1) + BK], ACT.Sign,
                                          bias=nsrcf[:, bass.ds(t, 1)], accum_out=n_sg[:, bass.ds(t, 1)])
                last.then_inc(sg_counted, 1)

            def normalise(c):
                act.wait_ge(rstd, c.n + 1)
                for r in range(R):
                    y = Y[:, c.par, r, :]
                    last = act.activation(y, y, ACT.Identity, bias=NM[:, c.par, r:r + 1], scale=RS[:, c.par, r:r + 1])
                last.then_inc(y_ready, 1)

            h1_half(Step(0, 0), 0)

            def slot_a(s):
                g = s.shift(-1)
                if s.within(G):
                    if s.past(0):
                        std_of(g)
                    c2_half(s, 0)
                    h1_half(s, 1)
                if g.within(G):
                    act.wait_ge(root_mm, g.n + 1)
                    if g.past(1):
                        act.wait_ge(root_out[g.par], g.turn * 16)
                    act.activation(RT[:, g.par, :], p_src[0:D, :], ACT.Identity, bias=b1c[:]).then_inc(root_act, 1)
                if s.within(G):
                    signs(s, 0)
                    if s.past(0):
                        normalise(g)
                    c2_half(s, 1)
                    h1_half(s.shift(1), 0)
                    signs(s, 1)
                if g.within(G):
                    act.wait_ge(row_turned, g.n + 1)
                    if g.past(1):
                        act.wait_ge(row_out[g.par], g.turn * 16)
                    act.activation(ROW[:, g.par, :, :], rows4(p_row), ACT.Copy).then_inc(row_ready, 1)
                if s.within(G):
                    act.wait_ge(src_turned, s.n + 1)
                    if s.past(1):
                        act.wait_ge(root_mm, s.n - 1)
                    act.activation(in_order(XS[0:D, s.par, :]), turned(p_src[0:D, :]), ACT.Copy).then_inc(xs_ready, 1)
                    act.wait_ge(dst_turned, s.n + 1)
                    if s.past(1):
                        act.wait_ge(rootd_mm, s.n - 1)
                    act.activation(XDT[:, s.par, :], p_dst[0:D, :], ACT.Copy).then_inc(xdt_ready, 1)

            run_slots(act, slot_a, 1, 1)

            def std_e_of(g):
                act.wait_ge(mean_var_e, g.n + 1)
                if g.past(1):
                    act.wait_ge(rstd_e, g.n - 1)
                act.activation(SDE[:, g.par, :], MVE[:, g.par, :, 1], ACT.Sqrt, bias=epsc[:]).then_inc(std_e, 1)

            def slot_b(s):
                c, g = s.shift(G), s.shift(-1)
                if s.within(G + 1):
                    std_of(c.shift(-1))
                if s.shift(-3).within(G):
                    std_e_of(s.shift(-3))
                if s.within(G):
                    c2_half(c, 0)
                    h1_half(c, 1)
                if s.within(G + 1):
                    normalise(c.shift(-1))
                if s.within(G):
                    c2_half(c, 1)
                    if s.within(G - 1):
                        h1_half(c.shift(1), 0)
                if g.within(G):
                    act.wait_ge(c2e_mm, g.n + 1)
                    if g.past(1):
                        act.wait_ge(ye_sum, g.n - 1)
                    act.activation(CE[:, g.par, :, :], rows4(p_row), ACT.Copy, scale=SLOPE).then_inc(c2e_act, 1)

            run_slots(act, slot_b, 2, 3)

        @block.vector
        def _(dve):
            chained = [0]

            def chain(ins):
                chained[0] += 1
                ins.then_inc(prep, 1)
                dve.wait_ge(prep, chained[0])

            dve.wait_ge(buckets_in, 48)
            chain(dve.tensor_tensor(runs[:], dstb[:], dstp[:], ALU.is_equal))
            chain(dve.tensor_scalar(runs[:], runs[:], 2.0, -1.0, ALU.mult, ALU.add))
            dve.tensor_scalar(runs[:], runs[:], FLT_MAX, None, ALU.mult).then_inc(runs_set, 1)
            dve.wait_ge(index_in, 48)
            dve.tensor_copy(srcf[:], srci[:])
            dve.tensor_scalar(nsrcf[:], srci[:], -1.0, None, ALU.mult).then_inc(src_set, 1)
            chain(dve.tensor_copy(pivot[:], dstb[:, 0:1]))
            chain(dve.memset(pivot[0:1, :], -1.0))
            chain(dve.tensor_tensor(steps[:, 0:BK], dstb[:], dsts[:], ALU.subtract))
            chain(dve.memset(steps[:, BK:BK + 1], float(BK)))
            dve.memset(steps[0:1, BK:BK + 1], 0.0).then_inc(look_set, 1)
            chain(dve.tensor_tensor(outf[:], dsti[:], dstn[:], ALU.is_equal))
            dve.scalar_tensor_tensor(out=outi[:], in0=outf[:], scalar=float(1 << 20), in1=dsti[:],
                                     op0=ALU.mult, op1=ALU.add).then_inc(outi_set, 1)
            dve.memset(H1[D:D + 1, :, :], 1.0)
            chain(dve.memset(HD[D:D + 1, :, :], 1.0))

            def leaky(t):
                return dve.scalar_tensor_tensor(out=t, in0=t, scalar=SLOPE, in1=t, op0=ALU.mult, op1=ALU.max)

            def h1_half(c, h):
                dve.wait_ge(h1_act, c.n * 2 + h + 1)
                leaky(H1[0:D, h, :]).then_inc(h1_leaky, 1)

            def c2_half(c, h):
                dve.wait_ge(c2_act, c.n * 2 + h + 1)
                dve.tensor_tensor(C2[:, h, :, :], rows4(p_c2), C2[:, h, :, :], ALU.max).then_inc(c2_leaky, 1)

            def y_half(c, h):
                dve.wait_ge(c2_leaky, c.n * 2 + h + 1)
                dve.wait_ge(x_turned, c.n * 2 + h + 1)
                if h == 0 and c.past(1):
                    dve.wait_ge(y_out[c.par], c.turn * 16)
                dve.tensor_tensor(Y[:, c.par, h * HR:(h + 1) * HR, :], rows4(p_x), C2[:, h, :, :], ALU.add)\
                   .then_inc(y_sum, 1)

            def stats_of(c):
                if c.past(0):
                    dve.wait_ge(mean_var, c.n)
                dve.wait_ge(y_sum, c.n * 2 + 2)
                dve.sem_inc(waited_dve, 1)
                for r in range(R):
                    last = dve.bn_stats(ST[:, r, :], Y[:, c.par, r, :])
                last.then_inc(stats, 1)
                dve.wait_ge(stats, c.n + 1)
                dve.sem_inc(waited_dve, 1)
                for r in range(R):
                    last = dve.bn_aggr(MV[:, c.par, r, :], ST[:, r, :])
                last.then_inc(mean_var, 1)

            def rstd_of(c):
                dve.wait_ge(std, c.n + 1)
                if c.past(1):
                    dve.wait_ge(y_ready, c.n - 1)
                dve.reciprocal(RS[:, c.par, :], SD[:, c.par, :]).then_inc(recip, 1)
                dve.wait_ge(recip, c.n + 1)
                dve.scalar_tensor_tensor(out=NM[:, c.par, :], in0=MV[:, c.par, :, 0], scalar=-1.0,
                                         in1=RS[:, c.par, :], op0=ALU.mult, op1=ALU.mult).then_inc(rstd, 1)

            def counts(g, j):
                dve.wait_ge(looked, g.n * 2 + j + 1)
                dve.wait_ge(sg_counted, g.n * 2 + j + 1)
                for i in range(2):
                    t = g.n * Q + 2 * j + i
                    at = i * (BK + 1)
                    dve.tensor_scalar(junk_v[:, i, :], p_look[:, at:at + BK], srcf[:, bass.ds(t, 1)], 0.0, ALU.is_le,
                                      ALU.add, accum_out=n_le[:, bass.ds(t, 1)])
                    last = dve.tensor_copy(n_bk[:, bass.ds(t, 1)], p_look[:, at + BK:at + BK + 1])
                last.then_inc(le_counted, 1)

            def scan(s, first):
                dve.wait_ge(msg_mm, s.n + 1)
                dve.wait_ge(run_in[s.par], (s.turn + 1) * 16)
                start = -FLT_MAX if first else SC[:, 1 - s.par, GE - 1:GE]
                if s.past(0):
                    dve.wait_ge(scanned, s.n)
                dve.tensor_tensor_scan(SC[:, s.par, :], RUN[:, s.par, :], p_msg[0:D, :], start, ALU.min, ALU.max)\
                   .then_inc(scanned, 1)

            def reach(g):
                dve.wait_ge(srcs_in[g.par], (g.turn + 1) * 16)
                if g.past(1):
                    dve.wait_ge(looked, g.n * 2 - 2)
                dve.tensor_scalar(GEQ[:, g.par, :], SB[:, g.par, :], pivot[:], None, ALU.is_ge)\
                   .then_inc(geq_ready, 1)

            reach(Step(0, 0))
            h1_half(Step(0, 0), 0)

            def slot_a(s):
                g = s.shift(-1)
                if s.within(G):
                    if s.past(0):
                        rstd_of(g)
                    c2_half(s, 0)
                    h1_half(s, 1)
                if g.within(G):
                    if g.past(1):
                        dve.wait_ge(row_turned, g.n - 1)
                    scan(g, not g.past(0))
                if s.within(G):
                    y_half(s, 0)
                if g.within(G):
                    dve.wait_ge(rootd_mm, g.n + 1)
                    dve.wait_ge(scanned, g.n + 1)
                    if g.past(1):
                        dve.wait_ge(hd_out[g.par], g.turn * 16)
                    dve.scalar_tensor_tensor(
                        out=HD[0:D, g.par, :].rearrange("m (q p) -> m q p", q=Q),
                        in0=p_dst[0:D, :].rearrange("m (q p) -> m q p", q=Q), scalar=b1c[:],
                        in1=SC[:, g.par, :].rearrange("m (p q) -> m q p", q=Q),
                        op0=ALU.add, op1=ALU.add).then_inc(hd_sum, 1)
                if s.within(G):
                    counts(s, 0)
                if g.within(G):
                    dve.wait_ge(hd_sum, g.n + 1)
                    leaky(HD[0:D, g.par, :]).then_inc(hd_ready, 1)
                if s.within(G):
                    c2_half(s, 1)
                    h1_half(s.shift(1), 0)
                    counts(s, 1)
                    if s.shift(1).within(G):
                        reach(s.shift(1))
                    y_half(s, 1)
                    stats_of(s)

            run_slots(dve, slot_a, 1, 1)

            dve.wait_ge(sg_counted, 2 * G)
            dve.wait_ge(le_counted, 2 * G)
            found, last = outf, srcf
            chain(dve.scalar_tensor_tensor(out=found[:], in0=n_le[:], scalar=2.0, in1=n_sg[:], op0=ALU.mult, op1=ALU.add))
            chain(dve.tensor_scalar(found[:], found[:], float(BK), None, ALU.is_gt))
            chain(dve.tensor_tensor(last[:], n_le[:], n_bk[:], ALU.add))
            chain(dve.tensor_scalar(last[:], last[:], float(-1 - EP), None, ALU.add))
            chain(dve.tensor_tensor(last[:], last[:], found[:], ALU.mult))
            dve.tensor_scalar(aggi[:], last[:], float(EP), None, ALU.add).then_inc(aggi_set, 1)
            for par, turns in ((0, G // 2 + 1), (1, G // 2)):
                dve.wait_ge(xd_kept[par], 16 * turns)
            dve.wait_ge(root_mm, G)
            dve.wait_ge(row_turned, G)

            def ye(g):
                return YE[:, bass.ds(g.n * Q, Q), :]

            def normalise_e(g):
                if g.past(0):
                    dve.wait_ge(ye_ready, g.n)
                dve.wait_ge(std_e, g.n + 1)
                dve.reciprocal(RSE[:], SDE[:, g.par, :]).then_inc(rstd_e, 1)
                dve.wait_ge(rstd_e, g.n + 1)
                for q in range(Q):
                    y = YE[:, bass.ds(g.n * Q + q, 1), :]
                    last = dve.tensor_scalar(y, y, MVE[:, g.par, q, 0:1], RSE[:, q:q + 1], ALU.subtract, ALU.mult)
                last.then_inc(ye_ready, 1)

            def leaky_e(g):
                dve.wait_ge(c2e_act, g.n + 1)
                dve.tensor_tensor(CE[:, g.par, :, :], rows4(p_row), CE[:, g.par, :, :], ALU.max)\
                   .then_inc(c2e_leaky, 1)

            def sum_e(g):
                dve.wait_ge(c2e_leaky, g.n + 1)
                dve.tensor_tensor(ye(g), ye(g), CE[:, g.par, :, :], ALU.add).then_inc(ye_sum, 1)
                if g.past(0):
                    dve.wait_ge(mean_var_e, g.n)
                dve.wait_ge(ye_sum, g.n + 1)
                dve.sem_inc(waited_dve, 1)
                for q in range(Q):
                    last = dve.bn_stats(STE[:, q, :], YE[:, bass.ds(g.n * Q + q, 1), :])
                last.then_inc(stats_e, 1)
                dve.wait_ge(stats_e, g.n + 1)
                dve.sem_inc(waited_dve, 1)
                for q in range(Q):
                    last = dve.bn_aggr(MVE[:, g.par, q, :], STE[:, q, :])
                last.then_inc(mean_var_e, 1)

            def slot_b(s):
                c, g = s.shift(G), s.shift(-1)
                if s.within(G + 1):
                    rstd_of(c.shift(-1))
                if s.shift(-2).within(G):
                    leaky_e(s.shift(-2))
                if s.within(G):
                    c2_half(c, 0)
                    h1_half(c, 1)
                if g.within(G):
                    if g.past(1):
                        dve.wait_ge(c2e_mm, g.n - 1)
                    scan(g.shift(G), not g.past(0))
                if s.within(G):
                    y_half(c, 0)
                if s.shift(-2).within(G):
                    sum_e(s.shift(-2))
                if s.shift(-3).within(G):
                    normalise_e(s.shift(-3))
                if s.within(G):
                    c2_half(c, 1)
                    if s.within(G - 1):
                        h1_half(c.shift(1), 0)
                    dve.wait_ge(src_turned, c.n + 1)
                    dve.wait_ge(root_in[s.par], (s.turn + 1) * 16)
                    dve.wait_ge(msg_mm, c.n - 1)
                    dve.tensor_tensor(in_order(XS[0:D, c.par, :]), turned(p_src[0:D, :]), in_order(RT[:, s.par, :]),
                                      ALU.add).then_inc(agg_sum, 1)
                    y_half(c, 1)
                    dve.wait_ge(agg_sum, s.n + 1)
                    leaky(XS[0:D, c.par, :]).then_inc(xs_ready, 1)
                    stats_of(c)

            run_slots(dve, slot_b, 2, 3)


def kernel(x, src, dst, edge_attr_32, L0_gnn_W1_msg, L0_gnn_W1_edge, L0_gnn_W1_root, L0_gnn_b1,
           L0_gnn_W2_msg, L0_gnn_W2_edge, L0_gnn_W2_root, L0_gnn_b2):
    import numpy as np
    import concourse.bacc as bacc
    from concourse.bass_utils import run_bass_kernel_spmd as run

    x, src, dst, ea = (np.asarray(a) for a in (x, src, dst, edge_attr_32))
    xrows = np.zeros((NP, D), x.dtype)
    xrows[:N] = x
    xcols = xrows.reshape(C, P, 2, HR, D).transpose(4, 0, 2, 3, 1).reshape(D, NP)
    ea_t = np.zeros((DE, EP), ea.dtype)
    ea_t[:, :E] = ea.T
    src_p = np.zeros(EP, src.dtype)
    src_p[:E] = src
    dst_p = np.full(EP + 1, N, dst.dtype)
    dst_p[:E] = dst
    dst_p[EP] = N + 1
    before = np.concatenate([np.full(1, -1, dst.dtype), dst_p[:EP - 1]])

    def by_group(a):
        return a.reshape(G, P, Q).transpose(1, 0, 2).reshape(P, G * Q)

    buckets = dst_p[:EP].reshape(P, BK)
    shifted = np.concatenate([np.zeros((1, BK), dst.dtype), buckets[:-1]])
    arrays = {
        "xrows": xrows, "xcols": xcols, "ea_t": ea_t,
        "src_q": by_group(src_p), "dst_q": by_group(dst_p[:EP]), "dst_next_q": by_group(dst_p[1:]),
        "src_flat": src_p, "dst_b": buckets, "dst_prev_b": before.reshape(P, BK), "dst_shift_b": shifted,
        "w1_msg": L0_gnn_W1_msg, "w1_edge": L0_gnn_W1_edge, "w1_root": L0_gnn_W1_root,
        "b1": np.asarray(L0_gnn_b1).reshape(D, 1),
        "w2_msg": L0_gnn_W2_msg, "w2_edge": L0_gnn_W2_edge, "w2_root": L0_gnn_W2_root,
        "b2": np.asarray(L0_gnn_b2).reshape(1, D),
    }
    nc = bacc.Bacc("TRN2", target_bir_lowering=False, num_devices=1)
    sent, args = {}, []
    for name, a in arrays.items():
        a = np.ascontiguousarray(a)
        sent[f"in_{name}"] = a
        args.append(nc.dram_tensor(f"in_{name}", a.shape, mybir.dt.from_np(a.dtype), kind="ExternalInput").ap())
    out = nc.dram_tensor("out_rows", (NP, D), F32, kind="ExternalOutput").ap()
    build(nc, *args, out)
    r = run(nc, [sent], core_ids=[0])
    return r.results[0]["out_rows"][:N]
```

```python
from contextlib import ExitStack

import concourse.bass as bass
from concourse import mybir

N, E, D, DE = 100000, 25000, 96, 32
P = 128
Q = 4
GE = P * Q
G = -(-E // GE)
EP = G * GE
R = 8
CN = P * R
C = -(-(N + 1) // CN)
NP = C * CN
HR = R // 2
HN = CN // 2
ACT_ROWS = 6
BK = EP // P
FLT_MAX = 3.4028234663852886e38
SLOPE = 0.01
EPS = 1e-5
assert C == 2 * G and G % 2 == 1 and HN == GE and EP > E and NP < 1 << 17

ALU = mybir.AluOpType
ACT = mybir.ActivationFunctionType
F32 = mybir.dt.float32
BF16 = mybir.dt.bfloat16
I32 = mybir.dt.int32


class Step:

    def __init__(self, k, o, k0=None):
        self.k, self.o, self.k0 = k, o, k if k0 is None else k0
        self.n = k * 2 + o
        self.par = o % 2
        self.turn = k + o // 2
        self.looped = k0 is not None

    def shift(self, d):
        return Step(self.k, self.o + d, self.k0 if self.looped else None)

    def past(self, d):
        assert not self.looped or 2 * self.k0 + self.o > d, "peel more ahead of the loop"
        return 2 * self.k0 + self.o > d

    def within(self, count):
        return self.looped or 0 <= self.n < count


def build(nc, xrows, xcols, ea_t, src_q, dst_q, dst_next_q, src_flat, dst_b, dst_prev_b, dst_shift_b,
          w1_msg, w1_edge, w1_root, b1, w2_msg, w2_edge, w2_root, b2, out):
    with ExitStack() as ctx:
        def sb(name, shape, dt=F32):
            return ctx.enter_context(nc.sbuf_tensor(name, shape, dt))

        def sem(name):
            return ctx.enter_context(nc.semaphore(name))

        def sem2(name):
            return [sem(name + "0"), sem(name + "1")]

        table1 = nc.dram_tensor("table1", [EP + 1, D], F32).ap()
        same_run = nc.dram_tensor("same_run", [EP], F32).ap()
        root_src = nc.dram_tensor("root_src", [G, D, GE], F32).ap()
        z1_dst = nc.dram_tensor("z1_dst", [G, D, GE], F32).ap()
        agg_src = nc.dram_tensor("agg_src", [G, P, Q * D], F32).ap()

        wm = [sb("wm1", [P, D]), sb("wm2", [P, D])]
        wr1 = sb("wr1", [P, D])
        wr2 = sb("wr2", [P, D])
        b1c = sb("b1c", [D, 1])
        w2s = sb("w2s", [P, D])
        b1s = sb("b1s", [D, 1])
        w1b_t = sb("w1b_t", [D, D + 1])
        w12x = sb("w12x", [P, D])
        w12 = sb("w12", [P, D])
        wr2x = sb("wr2x", [P, D])
        ident = sb("ident", [P, P])
        epsc = sb("epsc", [P, 1])
        zrow = sb("zrow", [1, D])

        srci = sb("srci", [P, G * Q], I32)
        dsti = sb("dsti", [P, G * Q], I32)
        dstn = sb("dstn", [P, G * Q], I32)
        srcf = sb("srcf", [P, G * Q])
        nsrcf = sb("nsrcf", [P, G * Q])
        outf = sb("outf", [P, G * Q])
        outi = sb("outi", [P, G * Q], I32)
        aggi = sb("aggi", [P, G * Q], I32)
        n_le = sb("n_le", [P, G * Q])
        n_sg = sb("n_sg", [P, G * Q])
        n_bk = sb("n_bk", [P, G * Q])
        dstb = sb("dstb", [P, BK], I32)
        dstp = sb("dstp", [P, BK], I32)
        dsts = sb("dsts", [P, BK], I32)
        pivot = sb("pivot", [P, 1])
        steps = sb("steps", [P, BK + 1])
        steps_hi = sb("steps_hi", [P, BK + 1], BF16)
        steps_lo = sb("steps_lo", [P, BK + 1], BF16)
        runs = sb("runs", [P, BK])
        idx_s = sb("idx_s", [P, 2, Q], I32)
        idx_d = sb("idx_d", [P, 2, Q], I32)
        idx_o = sb("idx_o", [P, 2, Q], I32)
        junk_v = sb("junk_v", [P, 2, BK])
        junk_a = sb("junk_a", [P, 2, BK])

        XT = sb("XT", [P, 2, CN])
        H1 = sb("H1", [P, 2, HN])
        C2 = sb("C2", [P, 2, HR, D])
        Y = sb("Y", [P, 2, R, D])
        YN = sb("YN", [P, 2, R, D])
        ST = sb("ST", [P, R, 6])
        MV = sb("MV", [P, 2, R, 2])
        SD = sb("SD", [P, 2, R])
        RS = sb("RS", [P, 2, R])
        NM = sb("NM", [P, 2, R])

        XG = sb("XG", [P, 2, Q, D])
        XD = sb("XD", [P, 2, Q, D])
        XS = sb("XS", [P, 2, GE])
        XDT = sb("XDT", [P, 2, GE])
        SB = sb("SB", [P, 2, GE], I32)
        GEQ = sb("GEQ", [P, 2, GE], BF16)
        RUN = sb("RUN", [D, 2, GE])
        SC = sb("SC", [P, 2, GE])
        RT = sb("RT", [D, 2, GE])
        HD = sb("HD", [P, 2, GE])
        HDR = sb("HDR", [P, 2, GE])
        ROW = sb("ROW", [P, 2, Q, D])
        CE = sb("CE", [P, 2, Q, D])
        YE = sb("YE", [P, G * Q, D])
        STE = sb("STE", [P, Q, 6])
        MVE = sb("MVE", [P, 2, Q, 2])
        SDE = sb("SDE", [P, 2, Q])
        RSE = sb("RSE", [P, 2, Q])
        NME = sb("NME", [P, 2, Q])
        OUTR = sb("OUTR", [P, 2, Q, D])

        def ps(name):
            return ctx.enter_context(nc.psum_tensor(name, [P, 512], F32))

        p_h1, p_c2, p_x = ps("p_h1"), ps("p_c2"), ps("p_x")
        p_src, p_dst, p_msg, p_row, p_look = ps("p_src"), ps("p_dst"), ps("p_msg"), ps("p_row"), ps("p_look")

        def turned(t):
            return t.rearrange("m (q p) -> m p q", q=Q)

        def in_order(t):
            return t.rearrange("m (p q) -> m p q", q=Q)

        def rows4(t):
            return t[:, 0:Q * D].rearrange("p (q f) -> p q f", q=Q)

        weights_in = sem("weights_in")
        index_in = sem("index_in")
        buckets_in = sem("buckets_in")
        xt_in = sem2("xt_in")
        ea_in = sem2("ea_in")
        run_in = sem2("run_in")
        srcs_in = sem2("srcs_in")
        root_in = sem2("root_in")
        hd_in = sem2("hd_in")
        xg_in = sem2("xg_in")
        xd_in = sem2("xd_in")
        runs_out = sem("runs_out")
        zero_out = sem("zero_out")
        row_out = sem2("row_out")
        root_out = sem2("root_out")
        hd_out = sem2("hd_out")
        y_out = sem2("y_out")
        xd_kept = sem2("xd_kept")
        agg_out = sem2("agg_out")
        agg_in = sem2("agg_in")
        scattered = sem2("scattered")
        const_set = sem("const_set")
        wr2_zeroed = sem("wr2_zeroed")
        pads_zeroed = sem("pads_zeroed")
        pads_set = sem("pads_set")
        ident_set = sem("ident_set")
        prep = sem("prep")
        runs_set = sem("runs_set")
        look_set = sem("look_set")
        src_set = sem("src_set")
        outi_set = sem("outi_set")
        aggi_set = sem("aggi_set")
        idx_copied = sem("idx_copied")
        idx_o_copied = sem("idx_o_copied")
        waited_pool = sem("waited_pool")
        waited_dve = sem("waited_dve")
        h1_mm = sem("h1_mm")
        h1_act = sem("h1_act")
        h1_leaky = sem("h1_leaky")
        x_turned = sem("x_turned")
        c2_mm = sem("c2_mm")
        c2_act = sem("c2_act")
        c2_leaky = sem("c2_leaky")
        y_sum = sem("y_sum")
        stats = sem("stats")
        mean_var = sem("mean_var")
        std = sem("std")
        recip = sem("recip")
        rstd = sem("rstd")
        y_ready = sem("y_ready")
        y_ready_v = sem("y_ready_v")
        w_turned = sem("w_turned")
        w_copied = sem("w_copied")
        w12_mm = sem("w12_mm")
        w12_set = sem("w12_set")
        w2s_set = sem("w2s_set")
        wr2x_set = sem("wr2x_set")
        src_turned = sem("src_turned")
        dst_turned = sem("dst_turned")
        xs_ready = sem("xs_ready")
        xdt_ready = sem("xdt_ready")
        msg_mm = sem("msg_mm")
        root_mm = sem("root_mm")
        rootd_mm = sem("rootd_mm")
        root_act = sem("root_act")
        geq_ready = sem("geq_ready")
        looked = sem("looked")
        le_counted = sem("le_counted")
        sg_counted = sem("sg_counted")
        scanned = sem("scanned")
        hd_sum = sem("hd_sum")
        hr_ready = sem("hr_ready")
        row_turned = sem("row_turned")
        row_ready = sem("row_ready")
        agg_sum = sem("agg_sum")
        c2e_mm = sem("c2e_mm")
        c2e_act = sem("c2e_act")
        c2e_leaky = sem("c2e_leaky")
        ye_sum = sem("ye_sum")
        stats_e = sem("stats_e")
        mean_var_e = sem("mean_var_e")
        std_e = sem("std_e")
        recip_e = sem("recip_e")
        rstd_e = sem("rstd_e")
        ye_ready = sem("ye_ready")

        block = ctx.enter_context(nc.Block())

        def run_slots(eng, slot, ahead, behind):
            for n in range(2 * ahead):
                slot(Step(n // 2, n % 2))
            with eng.Fori(ahead, G // 2) as k:
                slot(Step(k, 0, ahead))
                slot(Step(k, 1, ahead))
            for n in range(G - 1, G + behind):
                slot(Step(n // 2, n % 2))

        @block.sync
        def _(sp):
            sp.dma_start(srci[:], src_q).then_inc(index_in, 16)
            sp.dma_start(dsti[:], dst_q).then_inc(index_in, 16)
            sp.dma_start(dstn[:], dst_next_q).then_inc(index_in, 16)
            sp.dma_start(dstb[:], dst_b).then_inc(buckets_in, 16)
            sp.dma_start(dstp[:], dst_prev_b).then_inc(buckets_in, 16)
            sp.dma_start(dsts[:], dst_shift_b).then_inc(buckets_in, 16)
            sp.dma_start(wm[0][0:D, :], w1_msg).then_inc(weights_in, 16)
            sp.dma_start(wm[0][D:P, :], w1_edge).then_inc(weights_in, 16)
            sp.dma_start(wm[1][0:D, :], w2_msg).then_inc(weights_in, 16)
            sp.dma_start(wm[1][D:P, :], w2_edge).then_inc(weights_in, 16)
            sp.dma_start(wr1[0:D, :], w1_root).then_inc(weights_in, 16)
            sp.dma_start(wr2[0:D, :], w2_root).then_inc(weights_in, 16)
            sp.wait_ge(wr2_zeroed, 1)
            sp.dma_start(wr2[D:D + 1, :], b2).then_inc(weights_in, 16)
            sp.dma_start(b1c[:], b1).then_inc(weights_in, 16)
            sp.wait_ge(const_set, 1)
            sp.dma_start(table1[EP:EP + 1, :], zrow[:]).then_inc(zero_out, 16)
            sp.wait_ge(runs_set, 1)
            sp.dma_start(same_run.rearrange("(b j) -> b j", b=P), runs[:]).then_inc(runs_out, 16)
            sp.wait_ge(runs_out, 16)

            def load_dense(c):
                if c.past(1):
                    sp.wait_ge(x_turned, c.n * 2 - 2)
                sp.dma_start(XT[0:D, c.par, :], xcols[:, bass.ds(c.n * CN, CN)]).then_inc(xt_in[c.par], 16)

            def load_marks(s, g):
                if s.past(1):
                    sp.wait_ge(scanned, s.n - 1)
                sp.dma_start(RUN[:, s.par, :], same_run[bass.ds(g.n * GE, GE)].partition_broadcast(D))\
                  .then_inc(run_in[s.par], 16)

            def load_attributes(s, g):
                if s.past(1):
                    sp.wait_ge(msg_mm, s.n - 1)
                sp.dma_start(XS[D:P, s.par, :], ea_t[:, bass.ds(g.n * GE, GE)]).then_inc(ea_in[s.par], 16)

            def store_dense(c, split):
                sp.wait_ge(y_ready, c.n + 1)
                if split:
                    sp.wait_ge(y_ready_v, c.n + 1)
                sp.dma_start(out[bass.ds(c.n * CN, CN), :].rearrange("(p r) f -> p (r f)", p=P),
                             YN[:, c.par, :, :].rearrange("p r f -> p (r f)")).then_inc(y_out[c.par], 16)

            def keep_targets(g):
                sp.wait_ge(xd_in[g.par], (g.turn + 1) * 16 * Q)
                sp.dma_start(YE[:, bass.ds(g.n * Q, Q), :].rearrange("p q f -> p (q f)"),
                             XD[:, g.par, :, :].rearrange("p q f -> p (q f)")).then_inc(xd_kept[g.par], 16)

            def store_root(g):
                sp.wait_ge(root_act, g.n + 1)
                sp.dma_start(root_src[bass.ds(g.n, 1), :, :].rearrange("g d e -> d (g e)"),
                             RT[:, g.par, :]).then_inc(root_out[g.par], 16)

            def store_z1(g):
                sp.wait_ge(hd_sum, g.n + 1)
                sp.dma_start(z1_dst[bass.ds(g.n, 1), :, :].rearrange("g d e -> d (g e)"),
                             HD[0:D, g.par, :]).then_inc(hd_out[g.par], 16)

            def store_rows(g):
                sp.wait_ge(row_ready, g.n + 1)
                sp.dma_start(table1[bass.ds(g.n * GE, GE), :].rearrange("(p q) f -> p (q f)", p=P),
                             ROW[:, g.par, :, :].rearrange("p q f -> p (q f)")).then_inc(row_out[g.par], 16)

            def load_sources(g):
                if g.past(1):
                    sp.wait_ge(geq_ready, g.n - 1)
                sp.dma_start(SB[:, g.par, :], src_flat[bass.ds(g.n * GE, GE)].partition_broadcast(P))\
                  .then_inc(srcs_in[g.par], 16)

            load_dense(Step(0, 0))
            load_sources(Step(0, 0))

            def slot_a(s):
                g, c = s.shift(-1), s.shift(-3)
                if s.within(G):
                    load_marks(s, s)
                    load_attributes(s, s)
                if c.within(G):
                    store_dense(c, False)
                if g.within(G):
                    store_root(g)
                if s.within(G):
                    if s.past(0):
                        load_sources(s)
                    else:
                        load_dense(s.shift(1))
                if g.within(G):
                    store_rows(g)
                if s.within(G):
                    keep_targets(s)
                if g.within(G):
                    store_z1(g)
                if s.within(G) and s.past(0):
                    load_dense(s.shift(1))

            run_slots(sp, slot_a, 2, 3)

            def slot_b1(g):
                c = g.shift(G)
                if g.within(G - 1):
                    load_dense(c.shift(1))
                if g.within(G):
                    sp.wait_ge(xg_in[c.par], (c.turn + 1) * 16 * Q)
                    sp.dma_start(agg_src[bass.ds(g.n, 1), :, :].rearrange("g p f -> p (g f)"),
                                 XG[:, c.par, :, :].rearrange("p q f -> p (q f)")).then_inc(agg_out[c.par], 16)
                if g.shift(-2).within(G):
                    store_dense(c.shift(-2), True)

            run_slots(sp, slot_b1, 1, 0)
            for par, turns in ((0, G // 2 + 1), (1, G // 2)):
                sp.wait_ge(root_out[par], 16 * turns)
                sp.wait_ge(hd_out[par], 16 * turns)
                sp.wait_ge(agg_out[1 - par], 16 * turns)

            def slot_b2(g):
                e = g.shift(G)
                if g.past(1):
                    sp.wait_ge(agg_sum, g.n - 1)
                sp.dma_start(RT[:, g.par, :], root_src[bass.ds(g.n, 1), :, :].rearrange("g d e -> d (g e)"))\
                  .then_inc(root_in[g.par], 16)
                if g.past(1):
                    sp.wait_ge(src_turned, e.n - 1)
                sp.dma_start(XG[:, g.par, :, :].rearrange("p q f -> p (q f)"),
                             agg_src[bass.ds(g.n, 1), :, :].rearrange("g p f -> p (g f)")).then_inc(agg_in[g.par], 16)
                load_attributes(e, g)
                if g.past(1):
                    sp.wait_ge(c2e_mm, g.n - 1)
                sp.dma_start(HD[0:D, g.par, :], z1_dst[bass.ds(g.n, 1), :, :].rearrange("g d e -> d (g e)"))\
                  .then_inc(hd_in[g.par], 16)
                load_marks(e, g)
                if not g.past(1):
                    store_dense(Step(G - 1, g.n), True)

            run_slots(sp, slot_b2, 1, 0)
            for par in (0, 1):
                sp.wait_ge(y_out[par], 16 * G)

        @block.gpsimd
        def _(pool):
            pool.memset(zrow[:], 0.0).then_inc(const_set, 1)
            pool.memset(epsc[:], EPS).then_inc(ident_set, 1)
            pool.memset(ident[:], 0.0).then_inc(ident_set, 1)
            pool.wait_ge(ident_set, 2)
            pool.affine_select(out=ident[:], in_=ident[:], compare_op=ALU.not_equal, fill=1.0, base=0,
                               pattern=[[-1, P]], channel_multiplier=1).then_inc(ident_set, 1)
            pool.wait_ge(index_in, 48)

            def gather(to, rows, idx, par, bound, done):
                for q in range(Q):
                    pool.indirect_dma_start(
                        out=to[:, par, q, :], out_offset=None, in_=rows,
                        in_offset=bass.IndirectOffsetOnAxis(ap=idx[:, par, q:q + 1], axis=0),
                        bounds_check=bound, oob_is_err=False).then_inc(done[par], 16)

            def slot_a(g):
                if g.past(1):
                    pool.wait_ge(xg_in[g.par], g.turn * 16 * Q)
                    pool.wait_ge(xd_in[g.par], g.turn * 16 * Q)
                pool.tensor_copy(idx_s[:, g.par, :], srci[:, bass.ds(g.n * Q, Q)]).then_inc(idx_copied, 1)
                pool.tensor_copy(idx_d[:, g.par, :], dsti[:, bass.ds(g.n * Q, Q)]).then_inc(idx_copied, 1)
                pool.wait_ge(idx_copied, g.n * 2 + 2)
                if g.past(1):
                    pool.wait_ge(xd_kept[g.par], g.turn * 16)
                    pool.wait_ge(dst_turned, g.n - 1)
                pool.sem_inc(waited_pool, 1)
                gather(XD, xrows, idx_d, g.par, NP - 1, xd_in)
                if g.past(1):
                    pool.wait_ge(src_turned, g.n - 1)
                pool.sem_inc(waited_pool, 1)
                gather(XG, xrows, idx_s, g.par, NP - 1, xg_in)

            run_slots(pool, slot_a, 1, 0)
            for par, turns in ((0, G // 2 + 1), (1, G // 2)):
                pool.wait_ge(row_out[par], 16 * turns)
            pool.wait_ge(zero_out, 16)
            pool.wait_ge(aggi_set, 1)

            def slot_b(g):
                s = g.shift(G)
                pool.wait_ge(xg_in[s.par], s.turn * 16 * Q)
                pool.tensor_copy(idx_s[:, s.par, :], aggi[:, bass.ds(g.n * Q, Q)]).then_inc(idx_copied, 1)
                pool.wait_ge(idx_copied, g.n + 2 * G + 1)
                if g.past(1):
                    pool.wait_ge(agg_out[s.par], g.turn * 16)
                else:
                    pool.wait_ge(src_turned, G)
                pool.sem_inc(waited_pool, 1)
                gather(XG, table1, idx_s, s.par, EP, xg_in)

            run_slots(pool, slot_b, 1, 0)
            for par in (0, 1):
                pool.wait_ge(y_out[par], 16 * G)
            pool.wait_ge(outi_set, 1)

            def slot_c(g):
                pool.wait_ge(idx_o_copied, g.n + 1)
                pool.wait_ge(ye_ready, g.n + 1)
                pool.sem_inc(waited_pool, 1)
                for q in range(Q):
                    pool.indirect_dma_start(
                        out=out, out_offset=bass.IndirectOffsetOnAxis(ap=idx_o[:, g.par, q:q + 1], axis=0),
                        in_=OUTR[:, g.par, q, :], in_offset=None,
                        bounds_check=NP - 1, oob_is_err=False).then_inc(scattered[g.par], 16)

            run_slots(pool, slot_c, 1, 0)
            for par, turns in ((0, G // 2 + 1), (1, G // 2)):
                pool.wait_ge(scattered[par], 16 * Q * turns)

        @block.tensor
        def _(pe):
            pe.wait_ge(weights_in, 128)
            pe.wait_ge(ident_set, 3)
            pe.wait_ge(pads_set, 1)
            pe.transpose(p_c2[0:D, 0:D], wr1[0:D, :], ident[0:D, 0:D]).then_inc(w_turned, 1)
            pe.wait_ge(w_copied, 2)
            pe.matmul(p_c2[0:D + 1, 0:D], w1b_t[:], wr2[0:D, :], start=True, stop=True).then_inc(w12_mm, 1)
            pe.wait_ge(w12_set, 1)

            def h1_half(c, h, to=(p_h1, p_h1)):
                pe.wait_ge(xt_in[c.par], (c.turn + 1) * 16)
                if to[0] is not to[1]:
                    pe.wait_ge(h1_act, c.n * 2 + h - 1)
                elif c.past(0) or h:
                    pe.wait_ge(h1_act, c.n * 2 + h)
                pe.matmul(to[h][0:D, :], wr1[:], XT[:, c.par, h * HN:(h + 1) * HN], start=True, stop=True)\
                  .then_inc(h1_mm, 1)

            def x_half(c, h, to=(p_x, p_x)):
                pe.wait_ge(xt_in[c.par], (c.turn + 1) * 16)
                if to[0] is not to[1]:
                    pe.wait_ge(y_sum, c.n * 2 + h - 1)
                elif c.past(0) or h:
                    pe.wait_ge(y_sum, c.n * 2 + h)
                for r in range(HR):
                    last = pe.transpose(to[h][:, r * D:(r + 1) * D],
                                        XT[0:D, c.par, h * HN + r * P:h * HN + (r + 1) * P], ident[0:D, 0:D])
                last.then_inc(x_turned, 1)

            def c2_half(c, h):
                pe.wait_ge(h1_leaky, c.n * 2 + h + 1)
                if c.past(0) or h:
                    pe.wait_ge(c2_leaky, c.n * 2 + h)
                for r in range(HR):
                    last = pe.matmul(p_c2[:, r * D:(r + 1) * D], H1[:, h, r * P:(r + 1) * P], wr2[:],
                                     start=True, stop=True)
                last.then_inc(c2_mm, 1)

            def look_up(g, j):
                if g.past(0) or j:
                    pe.wait_ge(le_counted, g.n * 2 + j)
                    pe.wait_ge(sg_counted, g.n * 2 + j)
                for i in range(2):
                    q = 2 * j + i
                    to = p_look[:, i * (BK + 1):(i + 1) * (BK + 1)]
                    pe.matmul(to, GEQ[:, g.par, q::Q], steps_hi[:], start=True, stop=False)
                    last = pe.matmul(to, GEQ[:, g.par, q::Q], steps_lo[:], start=False, stop=True)
                last.then_inc(looked, 1)

            def turn_group(src, par, to, done):
                for q in range(Q):
                    last = pe.transpose(to[0:D, q * P:(q + 1) * P], src[:, par, q, :], ident[:])
                last.then_inc(done, 1)

            def slot_a(s):
                g = s.shift(-1)
                if s.within(G):
                    pe.wait_ge(xg_in[s.par], (s.turn + 1) * 16 * Q)
                    if s.past(0):
                        pe.wait_ge(root_act, s.n)
                    turn_group(XG, s.par, p_src, src_turned)
                    h1_half(s, 0)
                if g.within(G):
                    pe.wait_ge(geq_ready, g.n + 1)
                    pe.wait_ge(look_set, 1)
                    look_up(g, 0)
                    x_half(g, 1)
                if s.within(G):
                    pe.wait_ge(xs_ready, s.n + 1)
                    pe.wait_ge(ea_in[s.par], (s.turn + 1) * 16)
                    if s.past(0):
                        pe.wait_ge(scanned, s.n)
                    pe.matmul(p_msg[0:D, :], wm[0][:], XS[:, s.par, :], start=True, stop=True).then_inc(msg_mm, 1)
                    h1_half(s, 1)
                    pe.wait_ge(xd_in[s.par], (s.turn + 1) * 16 * Q)
                    if s.past(0):
                        pe.wait_ge(hd_sum, s.n)
                    turn_group(XD, s.par, p_dst, dst_turned)
                    c2_half(s, 0)
                    pe.matmul(p_src[0:D, :], wr1[0:D, :], XS[0:D, s.par, :], start=True, stop=True).then_inc(root_mm, 1)
                if g.within(G):
                    look_up(g, 1)
                if s.within(G):
                    pe.wait_ge(xdt_ready, s.n + 1)
                    pe.matmul(p_dst[0:D, :], wr1[:], XDT[:, s.par, :], start=True, stop=True).then_inc(rootd_mm, 1)
                    x_half(s, 0)
                    pe.wait_ge(scanned, s.n + 1)
                    if s.past(0):
                        pe.wait_ge(row_ready, s.n)
                    for q in range(Q):
                        last = pe.transpose(p_row[:, q * D:(q + 1) * D], SC[0:D, s.par, q::Q], ident[0:D, 0:D])
                    last.then_inc(row_turned, 1)
                    c2_half(s, 1)

            run_slots(pe, slot_a, 1, 1)

            h1_banks, c2_banks, x_banks = (p_h1, p_src), (p_c2, p_row), (p_x, p_dst)
            pe.wait_ge(root_act, G)
            pe.wait_ge(row_ready, G)
            pe.wait_ge(hd_sum, G)
            pe.wait_ge(wr2x_set, 1)

            def c2_half_b1(s, c, h):
                pe.wait_ge(c2_leaky, c.n * 2 + h - 1)
                if h:
                    pe.wait_ge(h1_leaky, s.n + 2 * G + 1)
                else:
                    pe.wait_ge(h1_act, c.n * 2 + 1)
                for r in range(HR):
                    to, part = c2_banks[h][:, r * D:(r + 1) * D], H1[:, h, r * P:(r + 1) * P]
                    if h:
                        last = pe.matmul(to, part, wr2[:], start=True, stop=True)
                    else:
                        pe.matmul(to, XT[:, c.par, r * P:(r + 1) * P], w12x[:], start=True, stop=False)
                        last = pe.matmul(to, part, wr2x[:], start=False, stop=True)
                last.then_inc(c2_mm, 1)

            def slot_b1(s):
                c = s.shift(G)
                for h in (0, 1):
                    h1_half(c, h, h1_banks)
                x_half(c, 0, x_banks)
                for h in (0, 1):
                    c2_half_b1(s, c, h)
                x_half(c, 1, x_banks)

            run_slots(pe, slot_b1, 1, 0)
            pe.wait_ge(h1_act, 2 * C)
            pe.wait_ge(c2_leaky, 2 * C)
            pe.wait_ge(w2s_set, 1)

            def slot_b2(s):
                r = s.shift(-1)
                if s.within(G):
                    pe.wait_ge(agg_in[s.par], (s.turn + 1) * 16)
                    if s.past(0):
                        pe.wait_ge(agg_sum, s.n)
                    turn_group(XG, s.par, p_src, src_turned)
                if r.within(G):
                    e = r.shift(G)
                    pe.wait_ge(scanned, e.n + 1)
                    pe.wait_ge(hr_ready, r.n + 1)
                    if r.past(0):
                        pe.wait_ge(c2e_leaky, r.n)
                    for q in range(Q):
                        to = p_row[:, q * D:(q + 1) * D]
                        pe.matmul(to, HDR[:, r.par, q * P:(q + 1) * P], wr2[:], start=True, stop=False)
                        pe.matmul(to, HD[:, r.par, q * P:(q + 1) * P], w2s[:], start=False, stop=False)
                        last = pe.matmul(to, SC[:, e.par, q::Q], ident[:, 0:D], start=False, stop=True)
                    last.then_inc(c2e_mm, 1)
                if s.within(G):
                    e = s.shift(G)
                    pe.wait_ge(xs_ready, e.n + 1)
                    pe.wait_ge(ea_in[e.par], (e.turn + 1) * 16)
                    pe.wait_ge(scanned, e.n)
                    pe.matmul(p_msg[0:D, :], wm[1][:], XS[:, e.par, :], start=True, stop=True).then_inc(msg_mm, 1)

            run_slots(pe, slot_b2, 1, 1)

        @block.scalar
        def _(act):
            act.wait_ge(weights_in, 128)
            act.wait_ge(ident_set, 3)
            act.wait_ge(src_set, 1)
            act.activation(b1s[:], b1c[:], ACT.Copy, scale=1.0 - SLOPE)
            act.activation(w1b_t[:, D:D + 1], b1c[:], ACT.Copy).then_inc(w_copied, 1)
            act.wait_ge(w_turned, 1)
            act.activation(w1b_t[:, 0:D], p_c2[0:D, 0:D], ACT.Copy).then_inc(w_copied, 1)
            act.wait_ge(w12_mm, 1)
            act.activation(w12[0:D + 1, :], p_c2[0:D + 1, 0:D], ACT.Copy, scale=SLOPE).then_inc(w12_set, 1)
            act.wait_ge(w12_set, 1)
            act.wait_ge(pads_zeroed, 1)
            act.activation(w2s[0:D, :], wr2[0:D, :], ACT.Copy, scale=SLOPE).then_inc(w2s_set, 1)

            def h1_half(c, h):
                act.wait_ge(h1_mm, c.n * 2 + h + 1)
                if c.past(0):
                    act.wait_ge(c2_mm, c.n * 2 + h - 1)
                act.activation(H1[0:D, h, :], p_h1[0:D, :], ACT.Identity, bias=b1c[:]).then_inc(h1_act, 1)

            def c2_half(c, h, bank=p_c2):
                act.wait_ge(c2_mm, c.n * 2 + h + 1)
                if c.past(0):
                    act.wait_ge(y_sum, c.n * 2 + h - 1)
                act.activation(C2[:, h, :, :], rows4(bank), ACT.Copy, scale=SLOPE).then_inc(c2_act, 1)

            def std_of(c):
                act.wait_ge(mean_var, c.n + 1)
                if c.past(1):
                    act.wait_ge(rstd, c.n - 1)
                act.activation(SD[:, c.par, :], MV[:, c.par, :, 1], ACT.Sqrt, bias=epsc[:]).then_inc(std, 1)

            def signs(g, j):
                act.wait_ge(looked, g.n * 2 + j + 1)
                for i in range(2):
                    t = g.n * Q + 2 * j + i
                    last = act.activation(junk_a[:, i, :], p_look[:, i * (BK + 1):i * (BK + 1) + BK], ACT.Sign,
                                          bias=nsrcf[:, bass.ds(t, 1)], accum_out=n_sg[:, bass.ds(t, 1)])
                last.then_inc(sg_counted, 1)

            def normalise(c, r0, r1, last_row=R):
                act.wait_ge(rstd, c.n + 1)
                if c.past(1):
                    act.wait_ge(y_out[c.par], c.turn * 16)
                for r in range(r0, r1):
                    last = act.activation(YN[:, c.par, r, :], Y[:, c.par, r, :], ACT.Identity,
                                          bias=NM[:, c.par, r:r + 1], scale=RS[:, c.par, r:r + 1])
                if r1 == last_row:
                    last.then_inc(y_ready, 1)

            def slot_a(s):
                g, c = s.shift(-1), s.shift(-2)
                if s.within(G):
                    act.wait_ge(src_turned, s.n + 1)
                    if s.past(1):
                        act.wait_ge(root_mm, s.n - 1)
                    act.activation(in_order(XS[0:D, s.par, :]), turned(p_src[0:D, :]), ACT.Copy).then_inc(xs_ready, 1)
                    h1_half(s, 0)
                if g.within(G):
                    signs(g, 0)
                if c.within(G):
                    normalise(c, HR, R)
                if s.within(G):
                    act.wait_ge(dst_turned, s.n + 1)
                    if s.past(1):
                        act.wait_ge(rootd_mm, s.n - 1)
                    act.activation(XDT[0:D, s.par, :], p_dst[0:D, :], ACT.Copy).then_inc(xdt_ready, 1)
                    h1_half(s, 1)
                    c2_half(s, 0)
                    act.wait_ge(root_mm, s.n + 1)
                    if s.past(1):
                        act.wait_ge(root_out[s.par], s.turn * 16)
                    act.activation(RT[:, s.par, :], p_src[0:D, :], ACT.Identity, bias=b1c[:]).then_inc(root_act, 1)
                if g.within(G):
                    std_of(g)
                    signs(g, 1)
                    normalise(g, 0, HR)
                if s.within(G):
                    c2_half(s, 1)
                    act.wait_ge(row_turned, s.n + 1)
                    if s.past(1):
                        act.wait_ge(row_out[s.par], s.turn * 16)
                    act.activation(ROW[:, s.par, :, :], rows4(p_row), ACT.Copy).then_inc(row_ready, 1)

            run_slots(act, slot_a, 2, 2)
            h1_banks, c2_banks = (p_h1, p_src), (p_c2, p_row)

            def h1_half_b1(c, h):
                act.wait_ge(h1_mm, c.n * 2 + h + 1)
                act.wait_ge(c2_mm, c.n * 2 + h - 1)
                if h:
                    act.activation(H1[0:D, h, :], h1_banks[h][0:D, :], ACT.Identity, bias=b1c[:]).then_inc(h1_act, 1)
                else:
                    act.activation(H1[0:D, h, :], h1_banks[h][0:D, :], ACT.Relu, bias=b1s[:], scale=1.0 - SLOPE)\
                       .then_inc(h1_act, 1)

            def slot_b1(s):
                c = s.shift(G)
                if s.within(G):
                    h1_half_b1(c, 0)
                    h1_half_b1(c, 1)
                if s.shift(-2).within(G):
                    normalise(c.shift(-2), 0, ACT_ROWS, ACT_ROWS)
                if s.within(G):
                    c2_half(c, 0, c2_banks[0])
                    c2_half(c, 1, c2_banks[1])
                if s.shift(-1).within(G):
                    std_of(c.shift(-1))

            run_slots(act, slot_b1, 1, 2)

            def std_e_of(g):
                act.wait_ge(mean_var_e, g.n + 1)
                if g.past(1):
                    act.wait_ge(rstd_e, g.n - 1)
                act.activation(SDE[:, g.par, :], MVE[:, g.par, :, 1], ACT.Sqrt, bias=epsc[:]).then_inc(std_e, 1)

            def normalise_e(g):
                act.wait_ge(rstd_e, g.n + 1)
                if g.past(1):
                    act.wait_ge(scattered[g.par], g.turn * 16 * Q)
                for q in range(Q):
                    last = act.activation(OUTR[:, g.par, q, :], YE[:, bass.ds(g.n * Q + q, 1), :], ACT.Identity,
                                          bias=NME[:, g.par, q:q + 1], scale=RSE[:, g.par, q:q + 1])
                last.then_inc(ye_ready, 1)

            def slot_b2(s):
                if s.within(G):
                    act.wait_ge(hd_in[s.par], (s.turn + 1) * 16)
                    if s.past(1):
                        act.wait_ge(c2e_mm, s.n - 1)
                    act.activation(HDR[0:D, s.par, :], HD[0:D, s.par, :], ACT.Relu, scale=1.0 - SLOPE)\
                       .then_inc(hr_ready, 1)
                if s.shift(-2).within(G):
                    normalise_e(s.shift(-2))
                if s.within(G):
                    act.wait_ge(c2e_mm, s.n + 1)
                    if s.past(1):
                        act.wait_ge(ye_sum, s.n - 1)
                    act.activation(CE[:, s.par, :, :], rows4(p_row), ACT.Copy, scale=SLOPE).then_inc(c2e_act, 1)
                if s.shift(-1).within(G):
                    std_e_of(s.shift(-1))

            run_slots(act, slot_b2, 2, 2)

        @block.vector
        def _(dve):
            dve.memset(wr2[D:P, :], 0.0).then_inc(wr2_zeroed, 1)
            for t in (XT, H1, XDT, SC, HD, HDR):
                dve.memset(t[D:P, :, :], 0.0)
            for t in (wr1, w12x, wr2x, w2s):
                last = dve.memset(t[D:P, :], 0.0)
            last.then_inc(pads_zeroed, 1)
            dve.wait_ge(pads_zeroed, 1)
            dve.memset(H1[D:D + 1, :, :], 1.0)
            dve.memset(HDR[D:D + 1, :, :], 1.0).then_inc(pads_set, 1)
            chained = [0]

            def chain(ins):
                chained[0] += 1
                ins.then_inc(prep, 1)
                dve.wait_ge(prep, chained[0])

            dve.wait_ge(buckets_in, 48)
            chain(dve.tensor_tensor(runs[:], dstb[:], dstp[:], ALU.is_equal))
            chain(dve.tensor_scalar(runs[:], runs[:], 2.0, -1.0, ALU.mult, ALU.add))
            dve.tensor_scalar(runs[:], runs[:], FLT_MAX, None, ALU.mult).then_inc(runs_set, 1)
            dve.wait_ge(index_in, 48)
            dve.tensor_copy(srcf[:], srci[:])
            dve.tensor_scalar(nsrcf[:], srci[:], -1.0, None, ALU.mult).then_inc(src_set, 1)
            chain(dve.tensor_copy(pivot[:], dstb[:, 0:1]))
            chain(dve.memset(pivot[0:1, :], -1.0))
            chain(dve.tensor_tensor(steps[:, 0:BK], dstb[:], dsts[:], ALU.subtract))
            chain(dve.memset(steps[:, BK:BK + 1], float(BK)))
            chain(dve.memset(steps[0:1, BK:BK + 1], 0.0))
            chain(dve.tensor_copy(steps_hi[:], steps[:]))
            dve.tensor_tensor(steps_lo[:], steps[:], steps_hi[:], ALU.subtract).then_inc(look_set, 1)
            chain(dve.tensor_tensor(outf[:], dsti[:], dstn[:], ALU.is_equal))
            dve.scalar_tensor_tensor(out=outi[:], in0=outf[:], scalar=float(1 << 20), in1=dsti[:],
                                     op0=ALU.mult, op1=ALU.add).then_inc(outi_set, 1)
            dve.wait_ge(w12_set, 1)
            dve.wait_ge(weights_in, 128)
            dve.wait_ge(pads_set, 1)
            dve.tensor_copy(wr2x[0:D, :], wr2[0:D, :])
            dve.tensor_copy(w12x[0:D, :], w12[0:D, :])
            dve.tensor_tensor(wr2x[D:D + 1, :], wr2[D:D + 1, :], w12[D:D + 1, :], ALU.add).then_inc(wr2x_set, 1)

            def leaky(t):
                return dve.scalar_tensor_tensor(out=t, in0=t, scalar=SLOPE, in1=t, op0=ALU.mult, op1=ALU.max)

            def h1_half(c, h):
                dve.wait_ge(h1_act, c.n * 2 + h + 1)
                leaky(H1[0:D, h, :]).then_inc(h1_leaky, 1)

            def c2_half(c, h, bank=p_c2):
                dve.wait_ge(c2_act, c.n * 2 + h + 1)
                dve.tensor_tensor(C2[:, h, :, :], rows4(bank), C2[:, h, :, :], ALU.max).then_inc(c2_leaky, 1)

            def y_half(c, h, bank=p_x):
                dve.wait_ge(c2_leaky, c.n * 2 + h + 1)
                dve.wait_ge(x_turned, c.n * 2 + h + 1)
                if h == 0 and c.past(1):
                    dve.wait_ge(y_ready, c.n - 1)
                dve.tensor_tensor(Y[:, c.par, h * HR:(h + 1) * HR, :], rows4(bank), C2[:, h, :, :], ALU.add)\
                   .then_inc(y_sum, 1)

            def stats_half(c, h):
                if h == 0 and c.past(0):
                    dve.wait_ge(mean_var, c.n)
                dve.wait_ge(y_sum, c.n * 2 + h + 1)
                dve.sem_inc(waited_dve, 1)
                for r in range(h * HR, (h + 1) * HR):
                    last = dve.bn_stats(ST[:, r, :], Y[:, c.par, r, :])
                last.then_inc(stats, 1)

            def mean_var_of(c):
                if c.past(1):
                    dve.wait_ge(y_ready, c.n - 1)
                dve.wait_ge(stats, c.n * 2 + 2)
                dve.sem_inc(waited_dve, 1)
                for r in range(R):
                    last = dve.bn_aggr(MV[:, c.par, r, :], ST[:, r, :])
                last.then_inc(mean_var, 1)

            def rstd_of(c):
                dve.wait_ge(std, c.n + 1)
                if c.past(1):
                    dve.wait_ge(y_ready, c.n - 1)
                dve.reciprocal(RS[:, c.par, :], SD[:, c.par, :]).then_inc(recip, 1)
                dve.wait_ge(recip, c.n + 1)
                dve.scalar_tensor_tensor(out=NM[:, c.par, :], in0=MV[:, c.par, :, 0], scalar=-1.0,
                                         in1=RS[:, c.par, :], op0=ALU.mult, op1=ALU.mult).then_inc(rstd, 1)

            def counts(g, j):
                dve.wait_ge(looked, g.n * 2 + j + 1)
                dve.wait_ge(sg_counted, g.n * 2 + j + 1)
                for i in range(2):
                    t = g.n * Q + 2 * j + i
                    at = i * (BK + 1)
                    dve.tensor_scalar(junk_v[:, i, :], p_look[:, at:at + BK], srcf[:, bass.ds(t, 1)], 0.0, ALU.is_le,
                                      ALU.add, accum_out=n_le[:, bass.ds(t, 1)])
                dve.tensor_copy(n_bk[:, bass.ds(g.n * Q + 2 * j, 2)], p_look[:, BK:2 * (BK + 1):BK + 1])\
                   .then_inc(le_counted, 1)

            def scan(s, first):
                dve.wait_ge(msg_mm, s.n + 1)
                dve.wait_ge(run_in[s.par], (s.turn + 1) * 16)
                start = -FLT_MAX if first else SC[0:D, 1 - s.par, GE - 1:GE]
                if s.past(0):
                    dve.wait_ge(scanned, s.n)
                dve.tensor_tensor_scan(SC[0:D, s.par, :], RUN[:, s.par, :], p_msg[0:D, :], start, ALU.min, ALU.max)\
                   .then_inc(scanned, 1)

            def reach(g):
                dve.wait_ge(srcs_in[g.par], (g.turn + 1) * 16)
                if g.past(1):
                    dve.wait_ge(looked, g.n * 2 - 2)
                dve.tensor_scalar(GEQ[:, g.par, :], SB[:, g.par, :], pivot[:], None, ALU.is_ge)\
                   .then_inc(geq_ready, 1)

            def slot_a(s):
                g = s.shift(-1)
                if s.within(G):
                    h1_half(s, 0)
                if g.within(G):
                    stats_half(g, 1)
                if s.within(G):
                    if s.past(1):
                        dve.wait_ge(row_turned, s.n - 1)
                    scan(s, not s.past(0))
                if g.within(G):
                    counts(g, 0)
                    mean_var_of(g)
                if s.within(G):
                    c2_half(s, 0)
                    h1_half(s, 1)
                if g.within(G):
                    rstd_of(g)
                if s.within(G):
                    reach(s)
                    dve.wait_ge(rootd_mm, s.n + 1)
                    dve.wait_ge(scanned, s.n + 1)
                    if s.past(1):
                        dve.wait_ge(hd_out[s.par], s.turn * 16)
                    dve.scalar_tensor_tensor(
                        out=HD[0:D, s.par, :].rearrange("m (q p) -> m q p", q=Q),
                        in0=p_dst[0:D, :].rearrange("m (q p) -> m q p", q=Q), scalar=b1c[:],
                        in1=SC[0:D, s.par, :].rearrange("m (p q) -> m q p", q=Q),
                        op0=ALU.add, op1=ALU.add).then_inc(hd_sum, 1)
                if g.within(G):
                    counts(g, 1)
                if s.within(G):
                    y_half(s, 0)
                    c2_half(s, 1)
                    stats_half(s, 0)
                    y_half(s, 1)

            run_slots(dve, slot_a, 2, 1)

            def normalise_b1(c):
                dve.wait_ge(rstd, c.n + 1)
                dve.wait_ge(y_out[c.par], c.turn * 16)
                for r in range(ACT_ROWS, R):
                    last = dve.tensor_scalar(YN[:, c.par, r, :], Y[:, c.par, r, :], RS[:, c.par, r:r + 1],
                                             NM[:, c.par, r:r + 1], ALU.mult, ALU.add)
                last.then_inc(y_ready_v, 1)

            c2_banks, x_banks = (p_c2, p_row), (p_x, p_dst)
            dve.sem_inc(y_ready_v, G)

            def slot_b1(s):
                c, b = s.shift(G), s.shift(G - 1)
                if s.within(G):
                    dve.wait_ge(h1_act, c.n * 2 + 2)
                    leaky(H1[0:D, 1, :]).then_inc(h1_leaky, 1)
                if s.shift(-1).within(G):
                    stats_half(b, 1)
                if s.shift(-2).within(G):
                    normalise_b1(c.shift(-2))
                if s.shift(-1).within(G):
                    mean_var_of(b)
                if s.within(G):
                    c2_half(c, 0, c2_banks[0])
                    c2_half(c, 1, c2_banks[1])
                    y_half(c, 0, x_banks[0])
                if s.shift(-1).within(G):
                    rstd_of(b)
                if s.within(G):
                    stats_half(c, 0)
                    y_half(c, 1, x_banks[1])

            dve.wait_ge(sg_counted, 2 * G)
            dve.wait_ge(le_counted, 2 * G)
            found, last = outf, srcf
            chain(dve.scalar_tensor_tensor(out=found[:], in0=n_le[:], scalar=2.0, in1=n_sg[:],
                                           op0=ALU.mult, op1=ALU.add))
            chain(dve.tensor_scalar(found[:], found[:], float(BK), None, ALU.is_gt))
            chain(dve.tensor_tensor(last[:], n_le[:], n_bk[:], ALU.add))
            chain(dve.tensor_scalar(last[:], last[:], float(-1 - EP), None, ALU.add))
            chain(dve.tensor_tensor(last[:], last[:], found[:], ALU.mult))
            dve.tensor_scalar(aggi[:], last[:], float(EP), None, ALU.add).then_inc(aggi_set, 1)
            run_slots(dve, slot_b1, 1, 2)
            for par, turns in ((0, G // 2 + 1), (1, G // 2)):
                dve.wait_ge(xd_kept[par], 16 * turns)
            dve.wait_ge(root_mm, G)
            dve.wait_ge(row_turned, G)

            def ye(g):
                return YE[:, bass.ds(g.n * Q, Q), :]

            def copy_rows_to(g):
                if g.past(1):
                    dve.wait_ge(scattered[g.par], g.turn * 16 * Q)
                dve.tensor_copy(idx_o[:, g.par, :], outi[:, bass.ds(g.n * Q, Q)]).then_inc(idx_o_copied, 1)

            def rstd_e_of(g):
                dve.wait_ge(std_e, g.n + 1)
                if g.past(1):
                    dve.wait_ge(ye_ready, g.n - 1)
                dve.reciprocal(RSE[:, g.par, :], SDE[:, g.par, :]).then_inc(recip_e, 1)
                dve.wait_ge(recip_e, g.n + 1)
                dve.scalar_tensor_tensor(out=NME[:, g.par, :], in0=MVE[:, g.par, :, 0], scalar=-1.0,
                                         in1=RSE[:, g.par, :], op0=ALU.mult, op1=ALU.mult).then_inc(rstd_e, 1)

            def leaky_e(g):
                dve.wait_ge(c2e_act, g.n + 1)
                dve.tensor_tensor(CE[:, g.par, :, :], rows4(p_row), CE[:, g.par, :, :], ALU.max)\
                   .then_inc(c2e_leaky, 1)

            def sum_e(g):
                dve.wait_ge(c2e_leaky, g.n + 1)
                dve.tensor_tensor(ye(g), ye(g), CE[:, g.par, :, :], ALU.add).then_inc(ye_sum, 1)

            def stats_e_of(g):
                if g.past(0):
                    dve.wait_ge(mean_var_e, g.n)
                dve.wait_ge(ye_sum, g.n + 1)
                dve.sem_inc(waited_dve, 1)
                for q in range(Q):
                    last = dve.bn_stats(STE[:, q, :], YE[:, bass.ds(g.n * Q + q, 1), :])
                last.then_inc(stats_e, 1)

            def mean_var_e_of(g):
                dve.wait_ge(stats_e, g.n + 1)
                dve.sem_inc(waited_dve, 1)
                for q in range(Q):
                    last = dve.bn_aggr(MVE[:, g.par, q, :], STE[:, q, :])
                last.then_inc(mean_var_e, 1)

            def slot_b2(s):
                r, t = s.shift(-1), s.shift(-2)
                if s.within(G):
                    e = s.shift(G)
                    dve.wait_ge(src_turned, e.n + 1)
                    dve.wait_ge(root_in[s.par], (s.turn + 1) * 16)
                    dve.wait_ge(msg_mm, e.n - 1)
                    dve.tensor_tensor(in_order(XS[0:D, e.par, :]), turned(p_src[0:D, :]), in_order(RT[:, s.par, :]),
                                      ALU.add).then_inc(agg_sum, 1)
                if t.within(G):
                    sum_e(t)
                if s.within(G):
                    dve.wait_ge(agg_sum, s.n + 1)
                    leaky(XS[0:D, e.par, :]).then_inc(xs_ready, 1)
                if t.within(G):
                    stats_e_of(t)
                    mean_var_e_of(t)
                if r.within(G):
                    leaky_e(r)
                if s.within(G):
                    if s.past(1):
                        dve.wait_ge(c2e_mm, s.n - 1)
                    scan(e, not s.past(0))
                if t.within(G):
                    copy_rows_to(t)
                    rstd_e_of(t)

            run_slots(dve, slot_b2, 2, 2)


def kernel(x, src, dst, edge_attr_32, L0_gnn_W1_msg, L0_gnn_W1_edge, L0_gnn_W1_root, L0_gnn_b1,
           L0_gnn_W2_msg, L0_gnn_W2_edge, L0_gnn_W2_root, L0_gnn_b2):
    import numpy as np
    import concourse.bacc as bacc
    from concourse.bass_utils import run_bass_kernel_spmd as run

    x, src, dst, ea = (np.asarray(a) for a in (x, src, dst, edge_attr_32))
    xrows = np.zeros((NP, D), x.dtype)
    xrows[:N] = x
    xcols = xrows.reshape(C, P, 2, HR, D).transpose(4, 0, 2, 3, 1).reshape(D, NP)
    ea_t = np.zeros((DE, EP), ea.dtype)
    ea_t[:, :E] = ea.T
    src_p = np.zeros(EP, src.dtype)
    src_p[:E] = src
    dst_p = np.full(EP + 1, N, dst.dtype)
    dst_p[:E] = dst
    dst_p[EP] = N + 1
    before = np.concatenate([np.full(1, -1, dst.dtype), dst_p[:EP - 1]])

    def by_group(a):
        return a.reshape(G, P, Q).transpose(1, 0, 2).reshape(P, G * Q)

    buckets = dst_p[:EP].reshape(P, BK)
    shifted = np.concatenate([np.zeros((1, BK), dst.dtype), buckets[:-1]])
    arrays = {
        "xrows": xrows, "xcols": xcols, "ea_t": ea_t,
        "src_q": by_group(src_p), "dst_q": by_group(dst_p[:EP]), "dst_next_q": by_group(dst_p[1:]),
        "src_flat": src_p, "dst_b": buckets, "dst_prev_b": before.reshape(P, BK), "dst_shift_b": shifted,
        "w1_msg": L0_gnn_W1_msg, "w1_edge": L0_gnn_W1_edge, "w1_root": L0_gnn_W1_root,
        "b1": np.asarray(L0_gnn_b1).reshape(D, 1),
        "w2_msg": L0_gnn_W2_msg, "w2_edge": L0_gnn_W2_edge, "w2_root": L0_gnn_W2_root,
        "b2": np.asarray(L0_gnn_b2).reshape(1, D),
    }
    nc = bacc.Bacc("TRN2", target_bir_lowering=False, num_devices=1)
    sent, args = {}, []
    for name, a in arrays.items():
        a = np.ascontiguousarray(a)
        sent[f"in_{name}"] = a
        args.append(nc.dram_tensor(f"in_{name}", a.shape, mybir.dt.from_np(a.dtype), kind="ExternalInput").ap())
    out = nc.dram_tensor("out_rows", (NP, D), F32, kind="ExternalOutput").ap()
    build(nc, *args, out)
    r = run(nc, [sent], core_ids=[0])
    return r.results[0]["out_rows"][:N]
```
